# Optimizing a Trainium2 kernel written in Bass

```python
import numpy as np
import jax
import jax.numpy as jnp

def _softmax(x, axis=-1):
    return jax.nn.softmax(x, axis=axis)

def _gelu(x):
    return jax.nn.gelu(x, approximate=True)

def _silu(x):
    return jax.nn.silu(x)

def _sigmoid(x):
    return jax.nn.sigmoid(x)

def _layernorm(x, axis=-1, eps=1e-05):
    m = jnp.mean(x, axis=axis, keepdims=True)
    v = jnp.var(x, axis=axis, keepdims=True)
    return (x - m) / jnp.sqrt(v + eps)

def _scatter_add(tgt, idx, src, axis=0):
    return tgt.at[idx].add(src)

def _segment_sum(src, seg, n):
    return jax.ops.segment_sum(src, seg, n)
kernel_name = 'mk_adaln_d1_jaxref_r8_6c0b95'

def setup_inputs(seed: int=0):
    np.random.seed(seed)
    _w = jnp.asarray

    def _L0_attn_setup():
        import jax, jax.numpy as jnp
        import numpy as np
        B, S, E, H = (2, 256, 256, 16)
        HD = E // H
        key = jax.random.key(seed)
        ks = jax.random.split(key, 7)
        inp = {'query': jax.random.normal(ks[0], (B, S, E), dtype=jnp.float32), 'key': jax.random.normal(ks[1], (B, S, E), dtype=jnp.float32), 'value': jax.random.normal(ks[2], (B, S, E), dtype=jnp.float32), 'Wqkv': jax.random.normal(ks[3], (3 * E, E), dtype=jnp.float32) * E ** (-0.5), 'bqkv': jnp.zeros((3 * E,), dtype=jnp.float32), 'Wproj': jax.random.normal(ks[4], (E, E), dtype=jnp.float32) * E ** (-0.5), 'bproj': jnp.zeros((E,), dtype=jnp.float32)}
        return inp
    _L0_attn_in = _L0_attn_setup()

    def _L0_ffn_setup():
        import jax, jax.numpy as jnp
        import numpy as np
        HIDDEN = 256
        INTER = 1024
        COMPRESSION = 128.9

        def _n_ctrl(out_size, in_size):
            return max(16, int(out_size * in_size / COMPRESSION))

        def _catmull_rom_grid(n_ctrl, n_samples):
            t = np.linspace(0.0, n_ctrl - 1.0, n_samples, dtype=np.float64)
            i = np.clip(np.floor(t).astype(np.int64), 0, n_ctrl - 2)
            f = (t - i).astype(np.float32)
            idx = np.stack([np.clip(i + k, 0, n_ctrl - 1) for k in (-1, 0, 1, 2)], axis=0)
            return (jnp.asarray(idx.astype(np.int32)), jnp.asarray(f))

        def spline_reconstruct(control_points, out_size, in_size):
            n = out_size * in_size
            idx, f = _catmull_rom_grid(control_points.shape[0], n)
            p0, p1, p2, p3 = (control_points[idx[0]], control_points[idx[1]], control_points[idx[2]], control_points[idx[3]])
            f2 = f * f
            f3 = f2 * f
            w = 0.5 * (2.0 * p1 + (p2 - p0) * f + (2.0 * p0 - 5.0 * p1 + 4.0 * p2 - p3) * f2 + (3.0 * p1 - p0 - 3.0 * p2 + p3) * f3)
            return w.reshape(out_size, in_size)
        key = jax.random.key(seed)
        k0, k1, k2, k3 = jax.random.split(key, 4)
        hidden_states = jax.random.normal(k0, (4, 256, HIDDEN), dtype=jnp.float32)
        gate_cp = jax.random.normal(k1, (_n_ctrl(INTER, HIDDEN),), dtype=jnp.float32) * 0.02
        up_cp = jax.random.normal(k2, (_n_ctrl(INTER, HIDDEN),), dtype=jnp.float32) * 0.02
        down_cp = jax.random.normal(k3, (_n_ctrl(HIDDEN, INTER),), dtype=jnp.float32) * 0.02
        return {'hidden_states': hidden_states, 'gate_cp': gate_cp, 'up_cp': up_cp, 'down_cp': down_cp}
    _L0_ffn_in = _L0_ffn_setup()
    _L0_c = _w((lambda *s: np.random.randn(*s).astype(np.float32) * 0.05)(2, 256))
    _L0_wmod = _w((lambda *s: np.random.randn(*s).astype(np.float32) * 0.05)(256, 6 * 256) * 256 ** (-0.5))
    _d = {'L0_attn_query': _L0_attn_in['query'], 'L0_attn_key': _L0_attn_in['key'], 'L0_attn_value': _L0_attn_in['value'], 'L0_attn_Wqkv': _L0_attn_in['Wqkv'], 'L0_attn_bqkv': _L0_attn_in['bqkv'], 'L0_attn_Wproj': _L0_attn_in['Wproj'], 'L0_attn_bproj': _L0_attn_in['bproj'], 'L0_ffn_gate_cp': _L0_ffn_in['gate_cp'], 'L0_ffn_up_cp': _L0_ffn_in['up_cp'], 'L0_ffn_down_cp': _L0_ffn_in['down_cp'], 'L0_c': _L0_c, 'L0_wmod': _L0_wmod}
    _x0 = _d['L0_attn_query']
    _d['L0_attn_query'] = jax.random.normal(jax.random.fold_in(jax.random.key(seed), 1), (2, 1024, 256), dtype=_x0.dtype)
    del _x0
    return _d

def reference(L0_attn_query, L0_attn_key, L0_attn_value, L0_attn_Wqkv, L0_attn_bqkv, L0_attn_Wproj, L0_attn_bproj, L0_ffn_gate_cp, L0_ffn_up_cp, L0_ffn_down_cp, L0_c, L0_wmod):

    def _L0_attn_ref(query, key, value, Wqkv, bqkv, Wproj, bproj):
        import jax, jax.numpy as jnp
        import numpy as np
        B, S, E, H = (2, 256, 256, 16)
        HD = E // H
        b, s, _ = query.shape
        qkv = query @ Wqkv.T + bqkv
        qkv = qkv.reshape(b, s, H, 3 * HD).transpose(0, 2, 1, 3)
        q = qkv[..., :HD]
        k = qkv[..., HD:2 * HD]
        v = qkv[..., 2 * HD:]
        scores = jnp.einsum('bhqd,bhkd->bhqk', q, k) * HD ** 0.5
        attn = jax.nn.softmax(scores, axis=-1)
        out = jnp.einsum('bhqk,bhkd->bhqd', attn, v)
        out = out.transpose(0, 2, 1, 3).reshape(b, s, E)
        return out @ Wproj.T + bproj

    def _L0_ffn_ref(hidden_states, gate_cp, up_cp, down_cp):
        import jax, jax.numpy as jnp
        import numpy as np
        HIDDEN = 256
        INTER = 1024
        COMPRESSION = 128.9

        def _n_ctrl(out_size, in_size):
            return max(16, int(out_size * in_size / COMPRESSION))

        def _catmull_rom_grid(n_ctrl, n_samples):
            t = np.linspace(0.0, n_ctrl - 1.0, n_samples, dtype=np.float64)
            i = np.clip(np.floor(t).astype(np.int64), 0, n_ctrl - 2)
            f = (t - i).astype(np.float32)
            idx = np.stack([np.clip(i + k, 0, n_ctrl - 1) for k in (-1, 0, 1, 2)], axis=0)
            return (jnp.asarray(idx.astype(np.int32)), jnp.asarray(f))

        def spline_reconstruct(control_points, out_size, in_size):
            n = out_size * in_size
            idx, f = _catmull_rom_grid(control_points.shape[0], n)
            p0, p1, p2, p3 = (control_points[idx[0]], control_points[idx[1]], control_points[idx[2]], control_points[idx[3]])
            f2 = f * f
            f3 = f2 * f
            w = 0.5 * (2.0 * p1 + (p2 - p0) * f + (2.0 * p0 - 5.0 * p1 + 4.0 * p2 - p3) * f2 + (3.0 * p1 - p0 - 3.0 * p2 + p3) * f3)
            return w.reshape(out_size, in_size)
        gate_w = spline_reconstruct(gate_cp, INTER, HIDDEN)
        up_w = spline_reconstruct(up_cp, INTER, HIDDEN)
        down_w = spline_reconstruct(down_cp, HIDDEN, INTER)
        gate = jnp.einsum('bsh,ih->bsi', hidden_states, gate_w)
        up = jnp.einsum('bsh,ih->bsi', hidden_states, up_w)
        inter = jax.nn.silu(gate) * up
        return jnp.einsum('bsi,hi->bsh', inter, down_w)
    x = L0_attn_query
    mod = (_silu(L0_c) @ L0_wmod).reshape(L0_c.shape[0], 6, 1, -1)
    sa, ca, ga, sb, cb, gb = (mod[:, 0], mod[:, 1], mod[:, 2], mod[:, 3], mod[:, 4], mod[:, 5])
    ga = (2 * (ga >= 0) - 1) * jnp.maximum(jnp.abs(ga), 0.25)
    gb = (2 * (gb >= 0) - 1) * jnp.maximum(jnp.abs(gb), 0.25)
    h = _layernorm(x, axis=-1) * (1 + ca) + sa
    x = x + ga * _L0_attn_ref(h, L0_attn_key, L0_attn_value, L0_attn_Wqkv, L0_attn_bqkv, L0_attn_Wproj, L0_attn_bproj)
    h = _layernorm(x, axis=-1) * (1 + cb) + sb
    x = x + gb * _L0_ffn_ref(h, L0_ffn_gate_cp, L0_ffn_up_cp, L0_ffn_down_cp)
    return x

_drawn_inputs = setup_inputs


def setup_inputs(seed=0):
    import zlib

    import numpy as np

    out = dict(_drawn_inputs(seed))
    spreads = {'L0_attn_bqkv': (0.0, 0.1), 'L0_attn_bproj': (0.0, 0.334)}
    factors = {'L0_ffn_gate_cp': 8.0, 'L0_ffn_up_cp': 8.0, 'L0_ffn_down_cp': 8.0}
    for name, (base, spread) in spreads.items():
        noise = np.random.default_rng([zlib.crc32(name.encode()), seed]).standard_normal(out[name].shape)
        drawn = base * np.exp(spread * noise) if base else spread * noise
        out[name] = jnp.asarray(drawn.astype(out[name].dtype))
    for name, factor in factors.items():
        out[name] = (out[name] * factor).astype(out[name].dtype)
    return out
```

```python
import concourse.bass as bass
from concourse import mybir
from concourse.alu_op_type import AluOpType as ALU
from contextlib import ExitStack

F32 = mybir.dt.float32
F32R = mybir.dt.float32r
BF16 = mybir.dt.bfloat16
ACT = mybir.ActivationFunctionType
AX = mybir.AxisListType.X

P = 128
B, S, E = 2, 1024, 256
H, HD = 16, 16
INTER = 1024
EK = E // P
IK = INTER // P
TILES = B * S // P
BLK = 512
BLOCKS = B * S // BLK
TPB = BLK // P
KT = S // P
GH = 4
GROUPS = B * H // GH
HALVES = S // BLK
STEPS = KT * HALVES
A_UNITS = GH * KT * HALVES
A_ALL = A_UNITS + 1
B_UNITS = GH * STEPS
RING = 3
Q_SLOTS = (0, 0, 0, 1, 1, 2)
K_SLOTS = (0, 1, 2, 0, 1, 0)
KROWS = HD * len(Q_SLOTS)
MROWS = 3
EPS = 1e-5
SCALE = float(HD) ** 0.5
N_CTRL = int(INTER * E / 128.9)
PIECES = INTER * E // (P * P)
A_PER_STEP = [5] * 8 + [4] * 6 + [0] * 2
assert sum(A_PER_STEP) == A_UNITS and len(A_PER_STEP) == STEPS
DMA = 16
START = 1


def adaln_block(nc, x_in, w_qkv, b_qkv, w_proj, b_proj, gate_cp, up_cp, down_cp, c_in, w_mod, phase, ramp, out):
    att_dram = nc.dram_tensor("attention_scratch", [4, P, S], F32).ap()
    den_dram = nc.dram_tensor("denominator_scratch", [4, 2 * GH, S], F32).ap()

    keep = ExitStack()
    with keep:
        def sb(name, shape, dt=F32, where=keep):
            return where.enter_context(nc.sbuf_tensor(name, shape, dt))

        def sem(name):
            return keep.enter_context(nc.semaphore(name))

        ps = keep.enter_context(nc.psum_tensor("ps", [P, 8, BLK], F32))

        ident = sb("ident", [P, P])
        ident_bf = sb("ident_bf", [P, P], BF16)
        affine = sb("affine", [P, 4, EK, B])
        gates = sb("gates", [P, B, 2, E])
        windows = sb("windows", [P, 3, PIECES, 5])
        phase_sb = sb("phase_sb", [P, PIECES])
        ramp_sb = sb("ramp_sb", [P, P])
        spline_w = sb("spline_w", [P, 3, PIECES, P])

        qkv_mem = ExitStack()
        q_parts = sb("q_parts", [P, 3, 2 * B * S], BF16, qkv_mem)
        k_parts = sb("k_parts", [P, 3, 2 * B * S], BF16, qkv_mem)
        v_all = sb("v_all", [P, 2, TILES, P], F32, qkv_mem)

        project_qkv(nc, locals())
        attention(nc, locals())
        qkv_mem.close()
        mlp(nc, locals())


def names(scope, *wanted):
    return [scope[n] for n in wanted]


def project_qkv(nc, scope):
    (sem, x_in, w_qkv, b_qkv, c_in, w_mod, gate_cp, up_cp, down_cp, phase, ramp, ps, ident, ident_bf, affine, gates,
     windows, phase_sb, ramp_sb, q_parts, k_parts, v_all) = names(
        scope, "sem", "x_in", "w_qkv", "b_qkv", "c_in", "w_mod", "gate_cp", "up_cp", "down_cp", "phase", "ramp", "ps",
        "ident", "ident_bf", "affine", "gates", "windows", "phase_sb", "ramp_sb", "q_parts", "k_parts", "v_all")
    FT = 6
    with ExitStack() as mem:
        def sb(name, shape, dt=F32):
            return mem.enter_context(nc.sbuf_tensor(name, shape, dt))

        x_sb = sb("x_sb", [P, TILES, E])
        xn = sb("xn", [P, TILES, E])
        w_rows = sb("w_rows", [P, FT, E])
        wt_hi = sb("wt_hi", [P, EK, FT * P], F32R)
        wt_lo = sb("wt_lo", [P, EK, FT * P], F32R)
        wm = sb("wm", [P, EK, 6 * E])
        c_t = sb("c_t", [P, EK, B])
        silu_c = sb("silu_c", [P, EK, B])
        silu_rep = sb("silu_rep", [P, EK, B, P])
        bias_qk = sb("bias_qk", [P, 2, 2])
        bias_v = sb("bias_v", [P, E])
        stats = sb("stats", [P, TILES, 6])
        mean_var = sb("mean_var", [P, TILES, 2])
        var_eps = sb("var_eps", [P, TILES])
        std = sb("std", [P, TILES])
        rstd0 = sb("rstd0", [P, TILES])
        newton = sb("newton", [P, TILES])
        rstd = sb("rstd", [P, TILES])
        h_full = sb("h_full", [P, 2, EK, BLK])
        h_hi = sb("h_hi", [P, 2, EK, BLK], F32R)
        h_lo = sb("h_lo", [P, 2, EK, BLK], F32R)
        qk_full = sb("qk_full", [P, 2, BLK])
        qk_rest = sb("qk_rest", [P, 2, BLK])
        gate_abs = sb("gate_abs", [P, B, 2 * E])
        gate_sign = sb("gate_sign", [P, B, 2 * E])

        x_loaded = [sem(f"x_loaded{i}") for i in range(BLOCKS)]
        w_loaded = sem("w_loaded")
        c_loaded = sem("c_loaded")
        wm_loaded = sem("wm_loaded")
        bias_loaded = sem("bias_loaded")
        spline_loaded = sem("spline_loaded")
        ident_ready = sem("ident_ready")
        pool_chain = sem("pool_chain")
        silu_ready = sem("silu_ready")
        silu_rep_ready = sem("silu_rep_ready")
        wt_made = sem("wt_made")
        wt_hi_ready = sem("wt_hi_ready")
        wt_ready = sem("wt_ready")
        mod_made = sem("mod_made")
        affine_ready = sem("affine_ready")
        gates_made = sem("gates_made")
        gates_ready = sem("gates_ready")
        dve_chain = sem("dve_chain")
        var_ready = sem("var_ready")
        std_ready = sem("std_ready")
        xn_ready = sem("xn_ready")
        xt_made = sem("xt_made")
        h_full_ready = sem("h_full_ready")
        h_hi_ready = sem("h_hi_ready")
        h_lo_ready = sem("h_lo_ready")
        qk_made = sem("qk_made")
        qk_full_ready = sem("qk_full_ready")
        part_h_ready = sem("part_h_ready")
        part_m_ready = sem("part_m_ready")
        part_l_ready = sem("part_l_ready")
        v_made = sem("v_made")
        v_ready = sem("v_ready")

        rows = w_qkv.rearrange("(h c d) e -> h c d e", c=3, d=HD)
        bias_rows = b_qkv.rearrange("(h c d) -> h c d", c=3, d=HD)
        wt_banks = [([(t, k, t * P) for t in range(4)], 0) for k in range(EK)]
        wt_banks = [[(t, 0) for t in range(4)], [(t, 1) for t in range(4)], [(4, 0), (5, 0), (4, 1), (5, 1)]]

        def wt_view(w, n):
            if n < 2:
                return w[:, n, 0:4 * P]
            return w[:, :, 4 * P:6 * P]

        def wt_psum(n):
            if n < 2:
                return ps[:, n, :]
            return ps[:, n, :].rearrange("p (k f) -> p k f", k=EK)

        with nc.Block() as block:

            @block.sync
            def _(sp):
                for comp in range(2):
                    for c in range(2):
                        for p in range(2):
                            src = rows[8 * c + 4 * p:8 * c + 4 * p + 4, comp].rearrange("j d e -> d j e")
                            sp.dma_start(w_rows[64 * p:64 * p + 64, 2 * comp + c, :], src).then_inc(w_loaded, DMA)
                for c in range(2):
                    sp.dma_start(w_rows[:, 4 + c, :], rows[8 * c:8 * c + 8, 2]).then_inc(w_loaded, DMA)
                with nc.allow_non_contiguous_dma(reason="biases by partition, once"):
                    for comp in range(2):
                        for c in range(2):
                            for p in range(2):
                                src = bias_rows[8 * c + 4 * p:8 * c + 4 * p + 4, comp].rearrange("j d -> d j")
                                sp.dma_start(bias_qk[64 * p:64 * p + 64, comp, c:c + 1], src).then_inc(bias_loaded, DMA)
                sp.dma_start(bias_v[:, :].rearrange("p (h d) -> p h d", d=HD),
                             bias_rows[:, 2, :].partition_broadcast(P)).then_inc(bias_loaded, DMA)
                for n, cp in enumerate((gate_cp, up_cp, down_cp)):
                    def piece(parts):
                        return bass.AP(cp.tensor, 0, [[1, parts], [P - 1, PIECES], [1, 5]])
                    sp.dma_start(windows[1:P, n], piece(P - 1)).then_inc(spline_loaded, DMA)
                    sp.dma_start(windows[0:1, n], piece(1)).then_inc(spline_loaded, DMA)
                sp.dma_start(phase_sb[:, :], phase).then_inc(spline_loaded, DMA)
                sp.dma_start(ramp_sb[:, :], ramp.partition_broadcast(P)).then_inc(spline_loaded, DMA)
                sp.wait_ge(bias_loaded, 9 * DMA)
                sp.wait_ge(spline_loaded, 8 * DMA)

            @block.gpsimd
            def _(pool):
                nc.gpsimd.memset(ident[:, :], 0.0).then_inc(pool_chain, 1)
                pool.wait_ge(pool_chain, 1)
                nc.gpsimd.affine_select(out=ident[:, :], in_=ident[:, :], compare_op=ALU.not_equal, fill=1.0,
                                        base=0, pattern=[[-1, P]], channel_multiplier=1).then_inc(pool_chain, 1)
                pool.wait_ge(pool_chain, 2)
                nc.gpsimd.tensor_copy(ident_bf[:, :], ident[:, :]).then_inc(ident_ready, 1)

                def h_low(i):
                    for k in range(EK):
                        pool.wait_ge(h_hi_ready, EK * i + k + 1)
                        if i >= 2:
                            pool.wait_ge(v_made, 2 * (i - 1))
                        nc.gpsimd.tensor_tensor(h_lo[:, i % 2, k], h_full[:, i % 2, k], h_hi[:, i % 2, k].bitcast(F32),
                                                ALU.subtract).then_inc(h_lo_ready, 1)

                h_low(0)
                for i in range(BLOCKS):
                    if i + 1 < BLOCKS:
                        h_low(i + 1)
                    for f in range(4):
                        n = 4 * i + f
                        parts = q_parts if f < 2 else k_parts
                        at = (f % 2) * B * S + i * BLK
                        pool.wait_ge(part_m_ready, n + 1)
                        nc.gpsimd.tensor_tensor(parts[:, 2, at:at + BLK], qk_rest[:, n % 2], parts[:, 1, at:at + BLK],
                                                ALU.subtract).then_inc(part_l_ready, 1)

            @block.scalar
            def _(act):
                with nc.allow_non_contiguous_dma(reason="the condition by partition, once"):
                    for b in range(B):
                        act.dma_start(c_t[:, :, b:b + 1].rearrange("p k b -> p (k b)"),
                                      c_in[b].rearrange("(k p) -> p k", p=P)).then_inc(c_loaded, DMA)
                for i in range(BLOCKS):
                    act.dma_start(x_sb[:, TPB * i:TPB * i + TPB],
                                  x_in[i * BLK:(i + 1) * BLK].rearrange("(t p) e -> p t e", p=P)).then_inc(x_loaded[i], DMA)
                    if i == 0:
                        act.dma_start(wm[:, :, :], w_mod.rearrange("(k p) f -> p k f", p=P)).then_inc(wm_loaded, DMA)
                act.wait_ge(c_loaded, B * DMA)
                nc.scalar.activation(silu_c[:, :, :], c_t[:, :, :], ACT.Silu).then_inc(silu_ready, 1)
                for n in range(3):
                    act.wait_ge(wt_made, n + 1)
                    nc.scalar.copy(wt_view(wt_hi, n), wt_psum(n)).then_inc(wt_hi_ready, 1)

                def h_affine(i):
                    act.wait_ge(var_ready, i + 1)
                    nc.scalar.activation(std[:, TPB * i:TPB * i + TPB], var_eps[:, TPB * i:TPB * i + TPB],
                                         ACT.Sqrt).then_inc(std_ready, 1)
                    if i == 0:
                        act.wait_ge(affine_ready, 1)
                    b = i // 2
                    for k in range(EK):
                        act.wait_ge(xt_made, EK * i + k + 1)
                        if i >= 2:
                            act.wait_ge(h_lo_ready, EK * (i - 1))
                        nc.scalar.activation(h_full[:, i % 2, k], ps[:, k, :], ACT.Identity, bias=affine[:, 0, k, b:b + 1],
                                             scale=affine[:, 1, k, b:b + 1]).then_inc(h_full_ready, 1)

                h_affine(0)
                for i in range(BLOCKS):
                    if i + 1 < BLOCKS:
                        h_affine(i + 1)
                    for f in range(4):
                        n = 4 * i + f
                        parts = q_parts if f < 2 else k_parts
                        at = (f % 2) * B * S + i * BLK
                        if n == 0:
                            act.wait_ge(bias_loaded, 9 * DMA)
                        act.wait_ge(qk_made, n + 1)
                        if n >= 2:
                            act.wait_ge(part_m_ready, n - 1)
                        nc.scalar.activation(qk_full[:, n % 2], ps[:, 2 + f, :], ACT.Identity,
                                             bias=bias_qk[:, f // 2, f % 2:f % 2 + 1]).then_inc(qk_full_ready, 1)
                        act.wait_ge(qk_full_ready, n + 1)
                        nc.scalar.copy(parts[:, 0, at:at + BLK], qk_full[:, n % 2]).then_inc(part_h_ready, 1)

            @block.vector
            def _(dve):
                done = [0]

                def link(ins):
                    done[0] += 1
                    ins.then_inc(dve_chain, 1)
                    dve.wait_ge(dve_chain, done[0])

                def layer_norm(i):
                    t0, t1 = TPB * i, TPB * i + TPB
                    dve.wait_ge(x_loaded[i], DMA)
                    for t in range(t0, t1):
                        last = nc.vector.bn_stats(stats[:, t], x_sb[:, t])
                    link(last)
                    for t in range(t0, t1):
                        last = nc.vector.bn_aggr(mean_var[:, t], stats[:, t])
                    link(last)
                    nc.vector.tensor_scalar(var_eps[:, t0:t1], mean_var[:, t0:t1, 1], EPS, None, ALU.add).then_inc(var_ready, 1)
                    dve.wait_ge(std_ready, i + 1)
                    link(nc.vector.reciprocal(rstd0[:, t0:t1], std[:, t0:t1]))
                    link(nc.vector.tensor_tensor(newton[:, t0:t1], rstd0[:, t0:t1], rstd0[:, t0:t1], ALU.mult))
                    link(nc.vector.tensor_tensor(newton[:, t0:t1], newton[:, t0:t1], var_eps[:, t0:t1], ALU.mult))
                    link(nc.vector.tensor_scalar(newton[:, t0:t1], newton[:, t0:t1], -0.5, 1.5, ALU.mult, ALU.add))
                    link(nc.vector.tensor_tensor(rstd[:, t0:t1], rstd0[:, t0:t1], newton[:, t0:t1], ALU.mult))
                    for t in range(t0, t1):
                        last = nc.vector.tensor_scalar(xn[:, t], x_sb[:, t], mean_var[:, t, 0:1], rstd[:, t:t + 1],
                                                       ALU.subtract, ALU.mult)
                    last.then_inc(xn_ready, 1)

                def h_high(i):
                    for k in range(EK):
                        dve.wait_ge(h_full_ready, EK * i + k + 1)
                        if i >= 2:
                            dve.wait_ge(v_made, 2 * (i - 1))
                        nc.vector.tensor_copy(h_hi[:, i % 2, k], h_full[:, i % 2, k]).then_inc(h_hi_ready, 1)

                dve.wait_ge(silu_ready, 1)
                nc.vector.tensor_copy(silu_rep[:, :, :, :],
                                      silu_c[:, :, :].unsqueeze(3).to_broadcast((P, EK, B, P))).then_inc(silu_rep_ready, 1)
                layer_norm(0)
                for n in range(3):
                    dve.wait_ge(wt_hi_ready, n + 1)
                    nc.vector.tensor_tensor(wt_view(wt_lo, n), wt_psum(n), wt_view(wt_hi, n).bitcast(F32),
                                            ALU.subtract).then_inc(wt_ready, 1)
                dve.wait_ge(mod_made, 1)
                mod = ps[:, 3, 0:4 * EK * B].rearrange("p (v k b) -> p v k b", v=4, k=EK)
                link(nc.vector.tensor_copy(affine[:, :, :, :], mod))
                nc.vector.tensor_scalar(affine[:, 1:4:2], affine[:, 1:4:2], 1.0, None, ALU.add).then_inc(affine_ready, 1)
                h_high(0)
                layer_norm(1)
                for i in range(BLOCKS):
                    if i + 1 < BLOCKS:
                        h_high(i + 1)
                    for f in range(4):
                        n = 4 * i + f
                        parts = q_parts if f < 2 else k_parts
                        at = (f % 2) * B * S + i * BLK
                        dve.wait_ge(part_h_ready, n + 1)
                        if n >= 2:
                            dve.wait_ge(part_l_ready, n - 1)
                        link(nc.vector.tensor_tensor(qk_rest[:, n % 2], qk_full[:, n % 2], parts[:, 0, at:at + BLK],
                                                     ALU.subtract))
                        nc.vector.tensor_copy(parts[:, 1, at:at + BLK], qk_rest[:, n % 2]).then_inc(part_m_ready, 1)
                    for half in range(2):
                        n = 2 * i + half
                        dve.wait_ge(v_made, n + 1)
                        if n == 0:
                            dve.wait_ge(bias_loaded, 9 * DMA)
                        t = TPB * i + 2 * half
                        nc.vector.tensor_tensor(
                            v_all[:, :, t:t + 2, :].rearrange("p c t f -> p t c f"),
                            ps[:, 6 + half, :].rearrange("p (t c f) -> p t c f", t=2, c=2),
                            bias_v[:, :].rearrange("p (c f) -> p c f", c=2).unsqueeze(1).to_broadcast((P, 2, 2, P)),
                            ALU.add).then_inc(v_ready, 1)
                    if i + 2 < BLOCKS:
                        layer_norm(i + 2)
                dve.wait_ge(gates_made, 1)
                for b in range(B):
                    link(nc.vector.tensor_scalar(gate_abs[:, b], ps[:, b, :], -1.0, 0.25, ALU.mult, ALU.max))
                    nc.vector.tensor_tensor(gate_abs[:, b], ps[:, b, :], gate_abs[:, b], ALU.max)
                    link(nc.vector.tensor_scalar(gate_sign[:, b], ps[:, b, :], 0.0, 2.0, ALU.is_ge, ALU.mult))
                for b in range(B):
                    nc.vector.scalar_tensor_tensor(
                        out=gates[:, b].rearrange("p g e -> p (g e)"), in0=gate_sign[:, b], scalar=-1.0,
                        in1=gate_abs[:, b], op0=ALU.add, op1=ALU.mult).then_inc(gates_ready, 1)

            @block.tensor
            def _(pe):
                pe.wait_ge(ident_ready, 1)
                pe.wait_ge(w_loaded, 10 * DMA)
                for n, pairs in enumerate(wt_banks):
                    for m, (t, k) in enumerate(pairs):
                        last = nc.tensor.transpose(ps[:, n, m * P:(m + 1) * P], w_rows[:, t, k * P:(k + 1) * P], ident[:, :])
                    last.then_inc(wt_made, 1)
                pe.wait_ge(silu_ready, 1)
                pe.wait_ge(wm_loaded, DMA)
                for v, column in enumerate((0, 1, 3, 4)):
                    for k in range(EK):
                        at = (v * EK + k) * B
                        for kk in range(EK):
                            last = nc.tensor.matmul(ps[:, 3, at:at + B],
                                                    wm[:, kk, column * E + k * P:column * E + (k + 1) * P],
                                                    silu_c[:, kk, :], start=(kk == 0), stop=(kk == EK - 1))
                last.then_inc(mod_made, 1)
                pe.wait_ge(wt_ready, 3)

                def transpose_block(i):
                    pe.wait_ge(xn_ready, i + 1)
                    if i:
                        pe.wait_ge(h_full_ready, EK * i)
                    for k in range(EK):
                        for t in range(TPB):
                            last = nc.tensor.transpose(ps[:, k, t * P:(t + 1) * P], xn[:, TPB * i + t, k * P:(k + 1) * P],
                                                       ident[:, :])
                        last.then_inc(xt_made, 1)

                transpose_block(0)
                pe.wait_ge(affine_ready, 1)
                for i in range(BLOCKS):
                    if i + 1 < BLOCKS:
                        transpose_block(i + 1)
                    pe.wait_ge(h_lo_ready, EK * (i + 1))
                    for f in range(4):
                        if i:
                            pe.wait_ge(qk_full_ready, 4 * (i - 1) + f + 1)
                        for k in range(EK):
                            for a, (w, h) in enumerate(((wt_hi, h_hi), (wt_hi, h_lo), (wt_lo, h_hi))):
                                last = nc.tensor.matmul(ps[:, 2 + f, :], w[:, k, f * P:(f + 1) * P], h[:, i % 2, k],
                                                        start=(k == 0 and a == 0), stop=(k == EK - 1 and a == 2))
                        last.then_inc(qk_made, 1)
                    for half in range(2):
                        if i:
                            pe.wait_ge(v_ready, 2 * (i - 1) + half + 1)
                        for t in range(2):
                            tok = slice((2 * half + t) * P, (2 * half + t + 1) * P)
                            for k in range(EK):
                                for a, (h, w) in enumerate(((h_hi, wt_hi), (h_hi, wt_lo), (h_lo, wt_hi))):
                                    last = nc.tensor.matmul(ps[:, 6 + half, t * E:(t + 1) * E], h[:, i % 2, k, tok],
                                                            w[:, k, 4 * P:6 * P],
                                                            start=(k == 0 and a == 0), stop=(k == EK - 1 and a == 2))
                        last.then_inc(v_made, 1)
                pe.wait_ge(silu_rep_ready, 1)
                pe.wait_ge(h_full_ready, EK * BLOCKS)
                for b in range(B):
                    for g, column in enumerate((2, 5)):
                        for kk in range(EK):
                            last = nc.tensor.matmul(ps[:, b, g * E:(g + 1) * E], silu_rep[:, kk, b, :],
                                                    wm[:, kk, column * E:(column + 1) * E],
                                                    start=(kk == 0), stop=(kk == EK - 1))
                last.then_inc(gates_made, 1)


def attention(nc, scope):
    (sem, ps, ident_bf, q_parts, k_parts, v_all, windows, phase_sb, ramp_sb, spline_w, att_dram, den_dram) = names(
        scope, "sem", "ps", "ident_bf", "q_parts", "k_parts", "v_all", "windows", "phase_sb", "ramp_sb", "spline_w",
        "att_dram", "den_dram")
    with ExitStack() as mem:
        def sb(name, shape, dt=F32):
            return mem.enter_context(nc.sbuf_tensor(name, shape, dt))

        qa = [sb(f"qa{p}", [KROWS, GH, S], BF16) for p in range(2)]
        ka = [sb(f"ka{p}", [KROWS, GH, S], BF16) for p in range(2)]
        qb = [sb(f"qb{p}", [KROWS + MROWS, GH, S], BF16) for p in range(2)]
        kb = [sb(f"kb{p}", [KROWS + MROWS, GH, S], BF16) for p in range(2)]
        vg = [sb(f"vg{p}", [P, KT, GH, 2 * HD]) for p in range(2)]
        probs = sb("probs", [P, 2, GH, BLK])
        heads = [sb(f"heads{p}", [P, HALVES, BLK]) for p in range(2)]
        max_parts = sb("max_parts", [P, GH * KT, HALVES])
        neg_max = sb("neg_max", [P, GH * KT])
        rest = sb("rest", [P, 2, GH * KT])
        neg_split = sb("neg_split", [P, MROWS, GH * KT], BF16)
        neg_rows = sb("neg_rows", [MROWS * GH * KT, P], BF16)
        coef = sb("coef", [P, 6, 3, PIECES])
        diff = sb("diff", [P, 3, PIECES, 10])
        z = sb("z", [P, 4, P])
        y = sb("y", [P, 4, P])
        bend = sb("bend", [P, 4, P])

        a_loaded = [sem(f"a_loaded{p}") for p in range(2)]
        b_loaded = [sem(f"b_loaded{p}") for p in range(2)]
        v_loaded = [sem(f"v_loaded{p}") for p in range(2)]
        max_loaded = [sem(f"max_loaded{p}") for p in range(2)]
        ones_ready = sem("ones_ready")
        a_full = sem("a_full")
        a_free = sem("a_free")
        neg_ready = sem("neg_ready")
        max_chain = sem("max_chain")
        b_full = sem("b_full")
        p_ready = sem("p_ready")
        pv_done = sem("pv_done")
        heads_ready = sem("heads_ready")
        heads_stored = [sem(f"heads_stored{p}") for p in range(2)]
        spline_chain = sem("spline_chain")

        SLOTS = len(Q_SLOTS)
        A_BANK, B_BANK, O_BANK = 0, RING, 2 * RING
        v_view = v_all[:, :, :, :].rearrange("p c (b k) (g j d) -> p (c b) k g (j d)", b=B, g=2, j=GH)
        neg_psum = ps[:, A_BANK + A_UNITS % RING, :].bitcast(BF16)[0:MROWS * GH * KT, 0:P]

        with nc.Block() as block:

            @block.sync
            def _(sp):
                def load_stack(q_to, k_to, at, p, loaded):
                    for to, parts, slots in ((q_to, q_parts, Q_SLOTS), (k_to, k_parts, K_SLOTS)):
                        for r, part in enumerate(slots):
                            sp.dma_start(to[HD * r:HD * r + HD], parts[64 * p:64 * p + 64, part, bass.ds(at, S)])\
                              .then_inc(loaded, DMA)

                def load_b(it, at, p):
                    load_stack(qb[p], kb[p], at, p, b_loaded[p])
                    for kt in range(KT):
                        sp.dma_start(vg[p][:, kt, :, 0:HD],
                                     v_view[:, bass.ds(it, 1), kt, p, :].rearrange("p o (j d) -> p (o j) d", j=GH))\
                          .then_inc(v_loaded[p], DMA)

                def load_max(p):
                    sp.dma_start(qb[p][KROWS:KROWS + MROWS], neg_rows[:, :]).then_inc(max_loaded[p], DMA)

                def store_heads(it, p):
                    for j in range(GH):
                        at = 64 * p + HD * j
                        sp.dma_start(att_dram[bass.ds(it, 1), at:at + HD, :], heads[p][32 * j:32 * j + HD])\
                          .then_inc(heads_stored[p], DMA)
                        sp.dma_start(den_dram[bass.ds(it, 1), GH * p + j:GH * p + j + 1, :],
                                     heads[p][32 * j + HD:32 * j + HD + 1]).then_inc(heads_stored[p], DMA)

                def in_register(value, most=1 << 16):
                    return sp.snap(sp.to_reg(value), min_val=0, max_val=most)

                def pair(it, number, last):
                    this, this_at = number(it, 2), number(it * S, 2 * S)
                    after, after_at = (None, None) if last else (number(it + 1, 3), number((it + 1) * S, 3 * S))
                    a_issued = [number((it * 2 + p + 1) * A_ALL) for p in range(2)]
                    pv_issued = [number((it * 2 + p) * STEPS + START) for p in range(2)]
                    a_read = [number((it * 2 + p + 2) * A_ALL) for p in range(2)]
                    heads_read = [number((it * 2 + p + 1) * HALVES + START) for p in range(2)]
                    for p in range(2):
                        sp.wait_ge(a_full, a_issued[p])
                        if not last:
                            load_stack(qa[p], ka[p], after_at, p, a_loaded[p])
                        if not last or p == 0:
                            sp.wait_ge(pv_done, pv_issued[p])
                            load_b(after if p else this, after_at if p else this_at, 1 - p)
                            sp.wait_ge(a_free, a_read[p])
                            load_max(1 - p)
                        sp.wait_ge(heads_ready, heads_read[p])
                        store_heads(this, p)

                for p in range(2):
                    sp.sem_inc(heads_stored[p], DMA)
                load_stack(qa[0], ka[0], 0, 0, a_loaded[0])
                load_b(0, 0, 0)
                load_stack(qa[1], ka[1], 0, 1, a_loaded[1])
                sp.wait_ge(a_free, A_ALL)
                load_max(0)
                with sp.Fori(0, GROUPS // 2 - 1) as it:
                    pair(it, in_register, False)
                pair(GROUPS // 2 - 1, lambda value, most=0: value, True)
                for p in range(2):
                    sp.wait_ge(heads_stored[p], GROUPS // 2 * 2 * GH * DMA + DMA)

            @block.tensor
            def _(pe):
                def a_unit(it, p, u):
                    g = it * 2 + p
                    j, t, half = u // (KT * HALVES), u // HALVES % KT, u % HALVES
                    if u == 0:
                        pe.wait_ge(a_loaded[p], (it + 1) * (2 * SLOTS * DMA))
                        pe.wait_ge(a_free, g * A_ALL)
                    if u >= RING:
                        pe.wait_ge(a_free, g * A_ALL + (u - RING + 1))
                    nc.tensor.matmul(ps[:, A_BANK + u % RING, :], qa[p][:, j, t * P:(t + 1) * P],
                                     ka[p][:, j, half * BLK:(half + 1) * BLK], start=True, stop=True).then_inc(a_full, 1)

                def max_transpose(it, p):
                    pe.wait_ge(neg_ready, it * 2 + (p + 1))
                    nc.tensor.transpose(neg_psum, neg_split[:, :, :].rearrange("p m u -> p (m u)"), ident_bf[:, :])\
                      .then_inc(a_full, 1)

                def b_unit(it, p, n, j):
                    g = it * 2 + p
                    u, kt, half = GH * n + j, n // HALVES, n % HALVES
                    if u == 0:
                        pe.wait_ge(b_loaded[p], (it + 1) * (2 * SLOTS * DMA))
                        pe.wait_ge(max_loaded[p], (it + 1) * DMA)
                    if u >= RING:
                        pe.wait_ge(p_ready, g * B_UNITS + (u - RING + 1))
                    nc.tensor.matmul(ps[:, B_BANK + u % RING, :], kb[p][:, j, kt * P:(kt + 1) * P],
                                     qb[p][:, j, half * BLK:(half + 1) * BLK], start=True, stop=True).then_inc(b_full, 1)

                def pv(it, p, n):
                    g = it * 2 + p
                    kt, half = n // HALVES, n % HALVES
                    if n == 0:
                        pe.wait_ge(v_loaded[p], (it + 1) * (KT * DMA))
                        pe.wait_ge(heads_ready, g * HALVES + START)
                    pe.wait_ge(p_ready, g * B_UNITS + GH * (n + 1))
                    for j in range(GH):
                        last = nc.tensor.matmul(ps[32 * j:32 * j + 32, O_BANK + half, :], vg[p][:, kt, j, :],
                                                probs[:, n % 2, j, :], start=(kt == 0), stop=(kt == KT - 1))
                    last.then_inc(pv_done, 1)

                def step(it, p, with_a):
                    it_a, p_a = it + p, 1 - p
                    u = 0
                    for n in range(STEPS):
                        for j in range(GH):
                            b_unit(it, p, n, j)
                            for _ in range(A_PER_STEP[n] * (j + 1) // GH - A_PER_STEP[n] * j // GH if with_a else 0):
                                a_unit(it_a, p_a, u)
                                u += 1
                        if n:
                            pv(it, p, n - 1)
                    pv(it, p, STEPS - 1)
                    if with_a:
                        max_transpose(it_a, p_a)

                pe.sem_inc(pv_done, START)
                pe.wait_ge(ones_ready, 4)
                for u in range(A_UNITS):
                    a_unit(0, 0, u)
                max_transpose(0, 0)
                with pe.Fori(0, GROUPS // 2 - 1) as it:
                    step(it, 0, True)
                    step(it, 1, True)
                step(GROUPS // 2 - 1, 0, True)
                step(GROUPS // 2 - 1, 1, False)

            @block.vector
            def _(dve):
                CHAIN = 5

                def maxima(g):
                    for u in range(A_UNITS):
                        dve.wait_ge(a_full, g * A_ALL + (u + 1))
                        nc.vector.tensor_reduce(max_parts[:, u // HALVES, u % HALVES:u % HALVES + 1],
                                                ps[:, A_BANK + u % RING, :], AX, ALU.max).then_inc(a_free, 1)
                    done = [0]

                    def link(ins):
                        done[0] += 1
                        ins.then_inc(max_chain, 1)
                        dve.wait_ge(max_chain, g * CHAIN + done[0])

                    dve.wait_ge(a_free, g * A_ALL + A_UNITS)
                    link(nc.vector.tensor_reduce(neg_max[:, :], max_parts[:, :, :], AX, ALU.max, negate=True))
                    link(nc.vector.tensor_copy(neg_split[:, 0], neg_max[:, :]))
                    link(nc.vector.tensor_tensor(rest[:, 0], neg_max[:, :], neg_split[:, 0], ALU.subtract))
                    link(nc.vector.tensor_copy(neg_split[:, 1], rest[:, 0]))
                    link(nc.vector.tensor_tensor(rest[:, 1], rest[:, 0], neg_split[:, 1], ALU.subtract))
                    assert done[0] == CHAIN
                    nc.vector.tensor_copy(neg_split[:, 2], rest[:, 1]).then_inc(neg_ready, 1)
                    dve.wait_ge(a_full, (g + 1) * A_ALL)
                    nc.vector.tensor_copy(neg_rows[:, :], neg_psum).then_inc(a_free, 1)

                for p in range(2):
                    nc.vector.memset(vg[p][:, :, :, HD:2 * HD], 1.0).then_inc(ones_ready, 1)
                for p in range(2):
                    nc.vector.memset(kb[p][KROWS:KROWS + MROWS], 1.0).then_inc(ones_ready, 1)
                maxima(0)
                with dve.Fori(0, GROUPS // 2 - 1) as it:
                    maxima(it * 2 + 1)
                    maxima(it * 2 + 2)
                maxima(GROUPS - 1)

            @block.scalar
            def _(act):
                def step(it, p):
                    g = it * 2 + p
                    for u in range(B_UNITS):
                        n, j = u // GH, u % GH
                        act.wait_ge(b_full, g * B_UNITS + (u + 1))
                        if u == 0:
                            act.wait_ge(pv_done, g * STEPS + START)
                        if j == 0 and n >= 2:
                            act.wait_ge(pv_done, g * STEPS + (n - 1 + START))
                        nc.scalar.activation(probs[:, n % 2, j, :], ps[:, B_BANK + u % RING, :], ACT.Exp,
                                             scale=SCALE).then_inc(p_ready, 1)
                    for half in range(HALVES):
                        act.wait_ge(pv_done, g * STEPS + (STEPS - HALVES + half + 1 + START))
                        if half == 0:
                            act.wait_ge(heads_stored[p], it * (2 * GH * DMA) + DMA)
                        nc.scalar.copy(heads[p][:, half, :], ps[:, O_BANK + half, :]).then_inc(heads_ready, 1)

                act.preload_act_table(ACT.Exp)
                act.sem_inc(heads_ready, START)
                with act.Fori(0, GROUPS // 2) as it:
                    step(it, 0)
                    step(it, 1)

            @block.gpsimd
            def _(pool):
                done = [0]

                def link(ins):
                    done[0] += 1
                    ins.then_inc(spline_chain, 1)
                    pool.wait_ge(spline_chain, done[0])

                def tt(to, a, b, op):
                    link(nc.gpsimd.tensor_tensor(to, a, b, op))

                pts, half_pts = windows[:, :, :, :], diff[:, :, :, 0:5]
                link(nc.gpsimd.tensor_scalar(half_pts, pts, 0.5, None, ALU.mult))
                d1, d2, d3 = diff[:, :, :, 5:9], diff[:, :, :, 0:3], diff[:, :, :, 3:5]
                tt(d1, diff[:, :, :, 1:5], diff[:, :, :, 0:4], ALU.subtract)
                tt(d2, d1[:, :, :, 1:4], d1[:, :, :, 0:3], ALU.subtract)
                tt(d3, d2[:, :, :, 1:3], d2[:, :, :, 0:2], ALU.subtract)
                c0 = windows[:, :, :, 1]
                c1, c2, c3, e2, e3 = (coef[:, n] for n in range(5))
                tt(c1, d1[:, :, :, 0], d1[:, :, :, 1], ALU.add)
                tt(c2, d2[:, :, :, 0], d3[:, :, :, 0], ALU.subtract)
                link(nc.gpsimd.tensor_copy(c3, d3[:, :, :, 0]))
                tt(e2, d3[:, :, :, 0], d3[:, :, :, 1], ALU.add)
                tt(e3, d3[:, :, :, 1], d3[:, :, :, 0], ALU.subtract)
                for q in range(PIECES // 4):
                    m = slice(4 * q, 4 * q + 4)

                    def wide(a):
                        return a.unsqueeze(2).to_broadcast((P, 4, P))

                    tt(z[:, :, :], ramp_sb[:, :].unsqueeze(1).to_broadcast((P, 4, P)), wide(phase_sb[:, m]), ALU.add)
                    link(nc.gpsimd.tensor_scalar(y[:, :, :], z[:, :, :], -1.0, None, ALU.add))
                    link(nc.gpsimd.tensor_scalar(y[:, :, :], y[:, :, :], 0.0, None, ALU.max))
                    for n in range(3):
                        w = spline_w[:, n, m, :]
                        tt(w, z[:, :, :], wide(c3[:, n, m]), ALU.mult)
                        tt(w, w, wide(c2[:, n, m]), ALU.add)
                        tt(w, w, z[:, :, :], ALU.mult)
                        tt(w, w, wide(c1[:, n, m]), ALU.add)
                        tt(w, w, z[:, :, :], ALU.mult)
                        tt(w, w, wide(c0[:, n, m]), ALU.add)
                        tt(bend[:, :, :], y[:, :, :], wide(e3[:, n, m]), ALU.mult)
                        tt(bend[:, :, :], bend[:, :, :], wide(e2[:, n, m]), ALU.subtract)
                        tt(bend[:, :, :], bend[:, :, :], y[:, :, :], ALU.mult)
                        tt(bend[:, :, :], bend[:, :, :], y[:, :, :], ALU.mult)
                        tt(w, w, bend[:, :, :], ALU.add)


def mlp(nc, scope):
    (sem, x_in, w_proj, b_proj, out, ps, ident, affine, gates, spline_w, att_dram, den_dram) = names(
        scope, "sem", "x_in", "w_proj", "b_proj", "out", "ps", "ident", "affine", "gates", "spline_w", "att_dram",
        "den_dram")
    with ExitStack() as mem:
        def sb(name, shape, dt=F32):
            return mem.enter_context(nc.sbuf_tensor(name, shape, dt))

        x_sb = sb("x_res", [P, TILES, E])
        wp = sb("wp", [P, EK, E])
        wp_hi = sb("wp_hi", [P, EK, E], F32R)
        wp_lo = sb("wp_lo", [P, EK, E], F32R)
        bp = sb("bp", [P, E])
        gu_hi = sb("gu_hi", [P, 2, EK, INTER], F32R)
        gu_lo = sb("gu_lo", [P, 2, EK, INTER], F32R)
        dn_hi = sb("dn_hi", [P, IK, E], F32R)
        dn_lo = sb("dn_lo", [P, IK, E], F32R)
        att = sb("att", [P, EK, BLK])
        den = sb("den", [P, EK, BLK])
        att_norm = sb("att_norm", [P, EK, BLK])
        att_hi = sb("att_hi", [P, EK, BLK], F32R)
        att_lo = sb("att_lo", [P, EK, BLK], F32R)
        xn = sb("xn2", [P, TPB, E])
        res = sb("res", [P, TPB, E])
        stats = sb("stats2", [P, TPB, 6])
        mean_var = sb("mean_var2", [P, TPB, 2])
        var_eps = sb("var_eps2", [P, TPB])
        std = sb("std2", [P, TPB])
        rstd0 = sb("rstd02", [P, TPB])
        newton = sb("newton2", [P, TPB])
        rstd = sb("rstd2", [P, TPB])
        h_full = sb("h_full2", [P, EK, BLK])
        h_hi = sb("h_hi2", [P, EK, BLK], F32R)
        h_lo = sb("h_lo2", [P, EK, BLK], F32R)
        silu = sb("silu", [P, 2, BLK])
        inter = sb("inter", [P, 2, BLK])
        in_hi = sb("in_hi", [P, IK, BLK], F32R)
        in_lo = sb("in_lo", [P, IK, BLK], F32R)
        y_sb = sb("y_sb", [P, TPB, E])

        wp_loaded = sem("wp_loaded")
        bp_loaded = sem("bp_loaded")
        x2_loaded = sem("x2_loaded")
        att_loaded = sem("att_loaded")
        tr_made = sem("tr_made")
        tr_hi = sem("tr_hi")
        tr_lo = sem("tr_lo")
        att_ready = sem("att_ready")
        proj_made = sem("proj_made")
        x1_ready = sem("x1_ready")
        chain = sem("mlp_chain")
        var_ready = sem("var_ready2")
        std_ready = sem("std_ready2")
        xn_ready = sem("xn_ready2")
        xt_made = sem("xt_made2")
        h_full_ready = sem("h_full_ready2")
        h_ready = sem("h_ready2")
        gu_made = sem("gu_made")
        silu_ready = sem("silu_ready2")
        in_ready = sem("in_ready")
        down_made = sem("down_made")
        y_ready = sem("y_ready")
        y_stored = sem("y_stored")

        G_BANK, D_BANK, X_BANK = 0, 4, 6
        TR = 3 * PIECES // 4 + 1
        tr_bank = [n % 4 for n in range(TR)]
        prod = lambda a, b: ((a[0], b[0]), (a[0], b[1]), (a[1], b[0]))

        def tr_out(n, w):
            if n == 0:
                return w[2][:, :, :].rearrange("p k (r e) -> p r k e", r=2)
            n -= 1
            weight, m = n // 4, 4 * (n % 4)
            if weight < 2:
                return w[0][:, weight, :, m * 64:(m + 4) * 64].rearrange("p k i -> p i k")
            return w[1][:, :, m * 16:(m + 4) * 16].rearrange("p i o -> p o i")

        def tr_in(n):
            bank = ps[:, tr_bank[n], :]
            if n == 0:
                return bank.rearrange("p (r k e) -> p r k e", r=2, k=EK)
            if (n - 1) // 4 < 2:
                return bank.rearrange("p (i k) -> p i k", k=EK)
            return bank.rearrange("p (o i) -> p o i", i=IK)

        with nc.Block() as block:

            @block.sync
            def _(sp):
                def load_att(i, b, half):
                    for c in range(EK):
                        part = b + 2 * c
                        sp.dma_start(att[:, c, :], att_dram[bass.ds(part, 1), :, bass.ds(half * BLK, BLK)])\
                          .then_inc(att_loaded, DMA)
                        for g in range(2 * GH):
                            sp.dma_start(den[HD * g:HD * g + HD, c, :],
                                         den_dram[bass.ds(part, 1), g, bass.ds(half * BLK, BLK)]
                                         .rearrange("o s -> (o s)").partition_broadcast(HD)).then_inc(att_loaded, DMA)

                sp.dma_start(wp[:, :, :], w_proj.rearrange("(r p) e -> p r e", p=P)).then_inc(wp_loaded, DMA)
                load_att(0, 0, 0)
                sp.dma_start(bp[:, :], b_proj.partition_broadcast(P)).then_inc(bp_loaded, DMA)
                sp.dma_start(x_sb[:, :, :], x_in.rearrange("(t p) e -> p t e", p=P)).then_inc(x2_loaded, DMA)

                def store(i):
                    sp.wait_ge(y_ready, i * 2 + 2 + START)
                    sp.dma_start(out[bass.ds(i * BLK, BLK), :].rearrange("(t p) e -> p t e", p=P), y_sb[:, :, :])\
                      .then_inc(y_stored, DMA)

                for i in range(BLOCKS):
                    if i + 1 < BLOCKS:
                        sp.wait_ge(att_ready, EK * (i + 1))
                        load_att(i + 1, (i + 1) // 2, (i + 1) % 2)
                    store(i)
                sp.wait_ge(y_stored, BLOCKS * DMA)

            @block.tensor
            def _(pe):
                pe.wait_ge(wp_loaded, DMA)
                for n in range(TR):
                    if n >= 4:
                        pe.wait_ge(tr_lo, n - 3)
                    for m in range(4):
                        if n == 0:
                            src = wp[:, m // 2, (m % 2) * P:(m % 2 + 1) * P]
                        else:
                            src = spline_w[:, (n - 1) // 4, 4 * ((n - 1) % 4) + m, :]
                        last = nc.tensor.transpose(ps[:, tr_bank[n], m * P:(m + 1) * P], src, ident[:, :])
                    last.then_inc(tr_made, 1)

                def project(i):
                    pe.wait_ge(att_ready, (i + 1) * EK)
                    for half in range(2):
                        for t in range(2):
                            tok = slice((2 * half + t) * P, (2 * half + t + 1) * P)
                            for k in range(EK):
                                for a, (x, w) in enumerate(prod((att_hi, att_lo), (wp_hi, wp_lo))):
                                    last = nc.tensor.matmul(ps[:, X_BANK + half, t * E:(t + 1) * E], x[:, k, tok], w[:, k, :],
                                                            start=(k == 0 and a == 0), stop=(k == EK - 1 and a == 2))
                        last.then_inc(proj_made, 1)

                def transpose_block(i):
                    pe.wait_ge(xn_ready, i + 1)
                    for k in range(EK):
                        for t in range(TPB):
                            last = nc.tensor.transpose(ps[:, X_BANK + k, t * P:(t + 1) * P], xn[:, t, k * P:(k + 1) * P],
                                                       ident[:, :])
                        last.then_inc(xt_made, 1)

                def gate_up(i):
                    pe.wait_ge(h_ready, (i + 1) * EK)
                    for c in range(IK):
                        if c >= 2:
                            pe.wait_ge(in_ready, i * IK + (c - 1))
                        for g in range(2):
                            for k in range(EK):
                                for a, (w, x) in enumerate(prod((gu_hi, gu_lo), (h_hi, h_lo))):
                                    last = nc.tensor.matmul(ps[:, G_BANK + 2 * (c % 2) + g, :],
                                                            w[:, g, k, c * P:(c + 1) * P], x[:, k, :],
                                                            start=(k == 0 and a == 0), stop=(k == EK - 1 and a == 2))
                        last.then_inc(gu_made, 1)

                def down(i):
                    pe.wait_ge(in_ready, (i + 1) * IK)
                    pe.wait_ge(y_ready, i * 2 + START)
                    for half in range(2):
                        for t in range(2):
                            tok = slice((2 * half + t) * P, (2 * half + t + 1) * P)
                            for c in range(IK):
                                for a, (x, w) in enumerate(prod((in_hi, in_lo), (dn_hi, dn_lo))):
                                    last = nc.tensor.matmul(ps[:, D_BANK + half, t * E:(t + 1) * E], x[:, c, tok], w[:, c, :],
                                                            start=(c == 0 and a == 0), stop=(c == IK - 1 and a == 2))
                        last.then_inc(down_made, 1)

                pe.wait_ge(tr_lo, TR)
                project(0)
                transpose_block(0)
                with pe.Fori(0, BLOCKS - 1) as i:
                    gate_up(i)
                    project(i + 1)
                    down(i)
                    transpose_block(i + 1)
                gate_up(BLOCKS - 1)
                down(BLOCKS - 1)

            @block.scalar
            def _(act):
                for n in range(TR):
                    act.wait_ge(tr_made, n + 1)
                    nc.scalar.copy(tr_out(n, (gu_hi, dn_hi, wp_hi)), tr_in(n)).then_inc(tr_hi, 1)

                def h_affine(i, b):
                    act.wait_ge(var_ready, i + 1)
                    nc.scalar.activation(std[:, :], var_eps[:, :], ACT.Sqrt).then_inc(std_ready, 1)
                    for k in range(EK):
                        act.wait_ge(xt_made, i * EK + (k + 1))
                        nc.scalar.activation(h_full[:, k], ps[:, X_BANK + k, :], ACT.Identity,
                                             bias=affine[:, 2, k, b:b + 1], scale=affine[:, 3, k, b:b + 1])\
                          .then_inc(h_full_ready, 1)

                h_affine(0, 0)
                for i in range(BLOCKS):
                    for c in range(IK):
                        act.wait_ge(gu_made, i * IK + (c + 1))
                        if i or c >= 2:
                            act.wait_ge(in_ready, i * IK + c - 1)
                        nc.scalar.activation(silu[:, c % 2], ps[:, G_BANK + 2 * (c % 2), :], ACT.Silu).then_inc(silu_ready, 1)
                    if i + 1 < BLOCKS:
                        h_affine(i + 1, (i + 1) // 2)

            @block.vector
            def _(dve):
                done = [0]

                def link(ins):
                    done[0] += 1
                    ins.then_inc(chain, 1)
                    dve.wait_ge(chain, done[0])

                def att_piece(i, piece):
                    c, part = piece // 4, piece % 4
                    if piece == 0:
                        dve.wait_ge(att_loaded, (i + 1) * (EK * (2 * GH + 1) * DMA))
                        if i:
                            dve.wait_ge(proj_made, 2 * i)
                    if part == 0:
                        link(nc.vector.reciprocal(den[:, c], den[:, c]))
                    elif part == 1:
                        link(nc.vector.tensor_tensor(att_norm[:, c], att[:, c], den[:, c], ALU.mult))
                    elif part == 2:
                        link(nc.vector.tensor_copy(att_hi[:, c], att_norm[:, c]))
                    else:
                        nc.vector.tensor_tensor(att_lo[:, c], att_norm[:, c], att_hi[:, c].bitcast(F32), ALU.subtract)\
                          .then_inc(att_ready, 1)

                def residual_and_norm(i, b):
                    gate = gates[:, b, 0, :].unsqueeze(1)
                    for half in range(2):
                        dve.wait_ge(proj_made, 2 * i + half + 1)
                        part = res[:, 2 * half:2 * half + 2, :]
                        x = x_sb[:, TPB * i + 2 * half:TPB * i + 2 * half + 2, :]
                        link(nc.vector.tensor_tensor(part, ps[:, X_BANK + half, :].rearrange("p (t e) -> p t e", t=2),
                                                     bp[:, :].unsqueeze(1).to_broadcast((P, 2, E)), ALU.add))
                        link(nc.vector.tensor_tensor(part, part, gate.to_broadcast((P, 2, E)), ALU.mult))
                        link(nc.vector.tensor_tensor(x, x, part, ALU.add))
                    for t in range(TPB):
                        last = nc.vector.bn_stats(stats[:, t], x_sb[:, TPB * i + t])
                    link(last)
                    for t in range(TPB):
                        last = nc.vector.bn_aggr(mean_var[:, t], stats[:, t])
                    link(last)
                    nc.vector.tensor_scalar(var_eps[:, :], mean_var[:, :, 1], EPS, None, ALU.add).then_inc(var_ready, 1)
                    dve.wait_ge(std_ready, i + 1)
                    link(nc.vector.reciprocal(rstd0[:, :], std[:, :]))
                    link(nc.vector.tensor_tensor(newton[:, :], rstd0[:, :], rstd0[:, :], ALU.mult))
                    link(nc.vector.tensor_tensor(newton[:, :], newton[:, :], var_eps[:, :], ALU.mult))
                    link(nc.vector.tensor_scalar(newton[:, :], newton[:, :], -0.5, 1.5, ALU.mult, ALU.add))
                    link(nc.vector.tensor_tensor(rstd[:, :], rstd0[:, :], newton[:, :], ALU.mult))
                    for t in range(TPB):
                        last = nc.vector.tensor_scalar(xn[:, t], x_sb[:, TPB * i + t], mean_var[:, t, 0:1], rstd[:, t:t + 1],
                                                       ALU.subtract, ALU.mult)
                    last.then_inc(xn_ready, 1)

                def h_parts(i):
                    for k in range(EK):
                        dve.wait_ge(h_full_ready, i * EK + k + 1)
                        link(nc.vector.tensor_copy(h_hi[:, k], h_full[:, k]))
                        nc.vector.tensor_tensor(h_lo[:, k], h_full[:, k], h_hi[:, k].bitcast(F32), ALU.subtract)\
                          .then_inc(h_ready, 1)

                dve.sem_inc(y_ready, START)
                for n in range(TR):
                    dve.wait_ge(tr_hi, n + 1)
                    nc.vector.tensor_tensor(tr_out(n, (gu_lo, dn_lo, wp_lo)), tr_in(n),
                                            tr_out(n, (gu_hi, dn_hi, wp_hi)).bitcast(F32), ALU.subtract).then_inc(tr_lo, 1)
                for piece in range(4 * EK):
                    att_piece(0, piece)
                dve.wait_ge(bp_loaded, DMA)
                dve.wait_ge(x2_loaded, DMA)
                residual_and_norm(0, 0)
                h_parts(0)
                for i in range(BLOCKS):
                    b = i // 2
                    for c in range(IK):
                        dve.wait_ge(silu_ready, i * IK + c + 1)
                        link(nc.vector.tensor_tensor(inter[:, c % 2], silu[:, c % 2], ps[:, G_BANK + 2 * (c % 2) + 1, :],
                                                     ALU.mult))
                        link(nc.vector.tensor_copy(in_hi[:, c], inter[:, c % 2]))
                        nc.vector.tensor_tensor(in_lo[:, c], inter[:, c % 2], in_hi[:, c].bitcast(F32), ALU.subtract)\
                          .then_inc(in_ready, 1)
                        if i + 1 < BLOCKS:
                            att_piece(i + 1, c)
                    if i + 1 < BLOCKS:
                        residual_and_norm(i + 1, (i + 1) // 2)
                    for half in range(2):
                        dve.wait_ge(down_made, 2 * i + half + 1)
                        if i and half == 0:
                            dve.wait_ge(y_stored, i * DMA)
                        part = res[:, 2 * half:2 * half + 2, :]
                        link(nc.vector.tensor_tensor(part, ps[:, D_BANK + half, :].rearrange("p (t e) -> p t e", t=2),
                                                     gates[:, b, 1, :].unsqueeze(1).to_broadcast((P, 2, E)), ALU.mult))
                        nc.vector.tensor_tensor(y_sb[:, 2 * half:2 * half + 2, :], part,
                                                x_sb[:, TPB * i + 2 * half:TPB * i + 2 * half + 2, :], ALU.add)\
                          .then_inc(y_ready, 1)
                    if i + 1 < BLOCKS:
                        h_parts(i + 1)


def _spline_grid(np):
    step = (N_CTRL - 1) / (INTER * E - 1)
    column, partition = np.meshgrid(np.arange(PIECES), np.arange(P))
    t = (P * (P * column + partition)) * step
    first = np.floor(t).astype(np.int64)
    assert (first == (P - 1) * column + np.maximum(partition - 1, 0)).all()
    return (t - first).astype(np.float32), (np.arange(P) * step).astype(np.float32)


def kernel(**inputs):
    import numpy as np
    import concourse.bacc as bacc
    from concourse.bass_utils import run_bass_kernel_spmd

    def ends_repeated(cp):
        cp = np.asarray(cp)
        return np.concatenate([cp[:1], cp, cp[-1:], cp[-1:]])

    phase, ramp = _spline_grid(np)
    arrays = {
        "x_in": np.ascontiguousarray(inputs["L0_attn_query"]).reshape(B * S, E),
        "w_qkv": np.ascontiguousarray(inputs["L0_attn_Wqkv"]),
        "b_qkv": np.ascontiguousarray(inputs["L0_attn_bqkv"]),
        "w_proj": np.ascontiguousarray(inputs["L0_attn_Wproj"]),
        "b_proj": np.ascontiguousarray(inputs["L0_attn_bproj"]),
        "gate_cp": ends_repeated(inputs["L0_ffn_gate_cp"]),
        "up_cp": ends_repeated(inputs["L0_ffn_up_cp"]),
        "down_cp": ends_repeated(inputs["L0_ffn_down_cp"]),
        "c_in": np.ascontiguousarray(inputs["L0_c"]),
        "w_mod": np.ascontiguousarray(inputs["L0_wmod"]),
        "phase": phase,
        "ramp": ramp,
    }
    nc = bacc.Bacc("TRN2", target_bir_lowering=False, num_devices=1)
    args = [nc.dram_tensor(name, a.shape, mybir.dt.from_np(a.dtype), kind="ExternalInput").ap()
            for name, a in arrays.items()]
    out = nc.dram_tensor("out", [B * S, E], F32, kind="ExternalOutput").ap()
    adaln_block(nc, *args, out)
    result = run_bass_kernel_spmd(nc, [arrays], core_ids=[0])
    return result.results[0]["out"].reshape(B, S, E)
```

```python
import concourse.bass as bass
from concourse import mybir
from concourse.alu_op_type import AluOpType as ALU
from contextlib import ExitStack

F32 = mybir.dt.float32
F32R = mybir.dt.float32r
BF16 = mybir.dt.bfloat16
ACT = mybir.ActivationFunctionType
AX = mybir.AxisListType.X

P = 128
B, S, E = 2, 1024, 256
H, HD = 16, 16
INTER = 1024
EK = E // P
IK = INTER // P
TILES = B * S // P
BLK = 512
BLOCKS = B * S // BLK
TPB = BLK // P
KT = S // P
GH = 4
GROUPS = B * H // GH
HALVES = S // BLK
STEPS = KT * HALVES
A_UNITS = GH * KT * HALVES
A_ALL = A_UNITS + 1
B_UNITS = GH * STEPS
RING = 3
Q_SLOTS = (0, 0, 0, 1, 1, 2)
K_SLOTS = (0, 1, 2, 0, 1, 0)
KROWS = HD * len(Q_SLOTS)
MROWS = 3
EPS = 1e-5
SCALE = float(HD) ** 0.5
N_CTRL = int(INTER * E / 128.9)
PIECES = INTER * E // (P * P)
A_AHEAD = 4
A_PER_STEP = [5, 4, 4] * 4 + [4] * 2
assert sum(A_PER_STEP) == A_UNITS - A_AHEAD and len(A_PER_STEP) == STEPS - 2
DMA = 16
START = 1


def adaln_block(nc, x_in, w_qkv, b_qkv, w_proj, b_proj, gate_cp, up_cp, down_cp, c_in, w_mod, phase, ramp, out):
    att_dram = nc.dram_tensor("attention_scratch", [4, P, S], F32).ap()
    den_dram = nc.dram_tensor("denominator_scratch", [4, 2 * GH, S], F32).ap()

    keep = ExitStack()
    with keep:
        def sb(name, shape, dt=F32, where=keep):
            return where.enter_context(nc.sbuf_tensor(name, shape, dt))

        def sem(name):
            return keep.enter_context(nc.semaphore(name))

        ps = keep.enter_context(nc.psum_tensor("ps", [P, 8, BLK], F32))

        ident = sb("ident", [P, P])
        ident_bf = sb("ident_bf", [P, P], BF16)
        affine = sb("affine", [P, 4, EK, B])
        gates = sb("gates", [P, B, 2, E])
        windows = sb("windows", [P, 3, PIECES, 5])
        phase_sb = sb("phase_sb", [P, PIECES])
        ramp_sb = sb("ramp_sb", [P, P])
        spline_w = sb("spline_w", [P, 3, PIECES, P])

        a_mem = sb("a_mem", [P, 2 * TILES * E])
        with ExitStack() as until_last_group:
            q_parts = sb("q_parts", [P, 3, 2 * B * S], BF16, until_last_group)
            k_parts = sb("k_parts", [P, 3, 2 * B * S], BF16, until_last_group)
            v_all = sb("v_all", [P, 2, TILES, P], F32, until_last_group)
        gu_hi = sb("gu_hi", [P, 2, EK, INTER], F32R)
        gu_lo = sb("gu_lo", [P, 2, EK, INTER], F32R)
        dn_hi = sb("dn_hi", [P, IK, E], F32R)
        dn_lo = sb("dn_lo", [P, IK, E], F32R)
        wp_hi = sb("wp_hi", [P, EK, E], F32R)
        wp_lo = sb("wp_lo", [P, EK, E], F32R)
        att_hi = sb("att_hi", [P, EK, BLK], F32R)
        att_lo = sb("att_lo", [P, EK, BLK], F32R)
        res = sb("res", [P, TPB, E])
        x_in_a, xn_in_a = (a_mem[:, h * TILES * E:(h + 1) * TILES * E].rearrange("p (t e) -> p t e", t=TILES)
                           for h in range(2))

        project_qkv(nc, locals())
        attention_and_mlp(nc, locals())


def names(scope, *wanted):
    return [scope[n] for n in wanted]


def project_qkv(nc, scope):
    (sem, x_in, w_qkv, b_qkv, c_in, w_mod, gate_cp, up_cp, down_cp, phase, ramp, ps, ident, ident_bf, affine, gates,
     windows, phase_sb, ramp_sb, q_parts, k_parts, v_all, x_sb, xn) = names(
        scope, "sem", "x_in", "w_qkv", "b_qkv", "c_in", "w_mod", "gate_cp", "up_cp", "down_cp", "phase", "ramp", "ps",
        "ident", "ident_bf", "affine", "gates", "windows", "phase_sb", "ramp_sb", "q_parts", "k_parts", "v_all",
        "x_in_a", "xn_in_a")
    FT = 6
    with ExitStack() as mem:
        def sb(name, shape, dt=F32):
            return mem.enter_context(nc.sbuf_tensor(name, shape, dt))

        w_rows = sb("w_rows", [P, FT, E])
        wt_hi = sb("wt_hi", [P, EK, FT * P], F32R)
        wt_lo = sb("wt_lo", [P, EK, FT * P], F32R)
        wm = sb("wm", [P, EK, 6 * E])
        c_t = sb("c_t", [P, EK, B])
        silu_c = sb("silu_c", [P, EK, B])
        silu_rep = sb("silu_rep", [P, EK, B, P])
        bias_qk = sb("bias_qk", [P, 2, 2])
        bias_v = sb("bias_v", [P, E])
        stats = sb("stats", [P, TILES, 6])
        mean_var = sb("mean_var", [P, TILES, 2])
        var_eps = sb("var_eps", [P, TILES])
        std = sb("std", [P, TILES])
        rstd0 = sb("rstd0", [P, TILES])
        newton = sb("newton", [P, TILES])
        rstd = sb("rstd", [P, TILES])
        h_full = sb("h_full", [P, 2, EK, BLK])
        h_hi = sb("h_hi", [P, 2, EK, BLK], F32R)
        h_lo = sb("h_lo", [P, 2, EK, BLK], F32R)
        qk_full = sb("qk_full", [P, 2, BLK])
        qk_rest = sb("qk_rest", [P, 2, BLK])
        gate_abs = sb("gate_abs", [P, B, 2 * E])
        gate_sign = sb("gate_sign", [P, B, 2 * E])

        x_loaded = [sem(f"x_loaded{i}") for i in range(BLOCKS)]
        w_loaded = sem("w_loaded")
        c_loaded = sem("c_loaded")
        wm_loaded = sem("wm_loaded")
        bias_loaded = sem("bias_loaded")
        spline_loaded = sem("spline_loaded")
        ident_ready = sem("ident_ready")
        pool_chain = sem("pool_chain")
        silu_ready = sem("silu_ready")
        silu_rep_ready = sem("silu_rep_ready")
        wt_made = sem("wt_made")
        wt_hi_ready = sem("wt_hi_ready")
        wt_ready = sem("wt_ready")
        mod_made = sem("mod_made")
        affine_ready = sem("affine_ready")
        gates_made = sem("gates_made")
        gates_ready = sem("gates_ready")
        dve_chain = sem("dve_chain")
        var_ready = sem("var_ready")
        std_ready = sem("std_ready")
        xn_ready = sem("xn_ready")
        xt_made = sem("xt_made")
        h_full_ready = sem("h_full_ready")
        h_hi_ready = sem("h_hi_ready")
        h_lo_ready = sem("h_lo_ready")
        qk_made = sem("qk_made")
        qk_full_ready = sem("qk_full_ready")
        part_h_ready = sem("part_h_ready")
        part_m_ready = sem("part_m_ready")
        part_l_ready = sem("part_l_ready")
        v_made = sem("v_made")
        v_ready = sem("v_ready")

        rows = w_qkv.rearrange("(h c d) e -> h c d e", c=3, d=HD)
        bias_rows = b_qkv.rearrange("(h c d) -> h c d", c=3, d=HD)
        wt_banks = [([(t, k, t * P) for t in range(4)], 0) for k in range(EK)]
        wt_banks = [[(t, 0) for t in range(4)], [(t, 1) for t in range(4)], [(4, 0), (5, 0), (4, 1), (5, 1)]]

        def wt_view(w, n):
            if n < 2:
                return w[:, n, 0:4 * P]
            return w[:, :, 4 * P:6 * P]

        def wt_psum(n):
            if n < 2:
                return ps[:, n, :]
            return ps[:, n, :].rearrange("p (k f) -> p k f", k=EK)

        with nc.Block() as block:

            @block.sync
            def _(sp):
                for comp in range(2):
                    for c in range(2):
                        for p in range(2):
                            src = rows[8 * c + 4 * p:8 * c + 4 * p + 4, comp].rearrange("j d e -> d j e")
                            sp.dma_start(w_rows[64 * p:64 * p + 64, 2 * comp + c, :], src).then_inc(w_loaded, DMA)
                for c in range(2):
                    sp.dma_start(w_rows[:, 4 + c, :], rows[8 * c:8 * c + 8, 2]).then_inc(w_loaded, DMA)
                with nc.allow_non_contiguous_dma(reason="biases by partition, once"):
                    for comp in range(2):
                        for c in range(2):
                            for p in range(2):
                                src = bias_rows[8 * c + 4 * p:8 * c + 4 * p + 4, comp].rearrange("j d -> d j")
                                sp.dma_start(bias_qk[64 * p:64 * p + 64, comp, c:c + 1], src).then_inc(bias_loaded, DMA)
                sp.dma_start(bias_v[:, :].rearrange("p (h d) -> p h d", d=HD),
                             bias_rows[:, 2, :].partition_broadcast(P)).then_inc(bias_loaded, DMA)
                for n, cp in enumerate((gate_cp, up_cp, down_cp)):
                    def piece(parts):
                        return bass.AP(cp.tensor, 0, [[1, parts], [P - 1, PIECES], [1, 5]])
                    sp.dma_start(windows[1:P, n], piece(P - 1)).then_inc(spline_loaded, DMA)
                    sp.dma_start(windows[0:1, n], piece(1)).then_inc(spline_loaded, DMA)
                sp.dma_start(phase_sb[:, :], phase).then_inc(spline_loaded, DMA)
                sp.dma_start(ramp_sb[:, :], ramp.partition_broadcast(P)).then_inc(spline_loaded, DMA)
                sp.wait_ge(bias_loaded, 9 * DMA)
                sp.wait_ge(spline_loaded, 8 * DMA)

            @block.gpsimd
            def _(pool):
                nc.gpsimd.memset(ident[:, :], 0.0).then_inc(pool_chain, 1)
                pool.wait_ge(pool_chain, 1)
                nc.gpsimd.affine_select(out=ident[:, :], in_=ident[:, :], compare_op=ALU.not_equal, fill=1.0,
                                        base=0, pattern=[[-1, P]], channel_multiplier=1).then_inc(pool_chain, 1)
                pool.wait_ge(pool_chain, 2)
                nc.gpsimd.tensor_copy(ident_bf[:, :], ident[:, :]).then_inc(ident_ready, 1)

                def h_low(i):
                    for k in range(EK):
                        pool.wait_ge(h_hi_ready, EK * i + k + 1)
                        if i >= 2:
                            pool.wait_ge(v_made, 2 * (i - 1))
                        nc.gpsimd.tensor_tensor(h_lo[:, i % 2, k], h_full[:, i % 2, k], h_hi[:, i % 2, k].bitcast(F32),
                                                ALU.subtract).then_inc(h_lo_ready, 1)

                h_low(0)
                for i in range(BLOCKS):
                    if i + 1 < BLOCKS:
                        h_low(i + 1)
                    for f in range(4):
                        n = 4 * i + f
                        parts = q_parts if f < 2 else k_parts
                        at = (f % 2) * B * S + i * BLK
                        pool.wait_ge(part_m_ready, n + 1)
                        nc.gpsimd.tensor_tensor(parts[:, 2, at:at + BLK], qk_rest[:, n % 2], parts[:, 1, at:at + BLK],
                                                ALU.subtract).then_inc(part_l_ready, 1)

            @block.scalar
            def _(act):
                with nc.allow_non_contiguous_dma(reason="the condition by partition, once"):
                    for b in range(B):
                        act.dma_start(c_t[:, :, b:b + 1].rearrange("p k b -> p (k b)"),
                                      c_in[b].rearrange("(k p) -> p k", p=P)).then_inc(c_loaded, DMA)
                for i in range(BLOCKS):
                    act.dma_start(x_sb[:, TPB * i:TPB * i + TPB],
                                  x_in[i * BLK:(i + 1) * BLK].rearrange("(t p) e -> p t e", p=P)).then_inc(x_loaded[i], DMA)
                    if i == 0:
                        act.dma_start(wm[:, :, :], w_mod.rearrange("(k p) f -> p k f", p=P)).then_inc(wm_loaded, DMA)
                act.wait_ge(c_loaded, B * DMA)
                nc.scalar.activation(silu_c[:, :, :], c_t[:, :, :], ACT.Silu).then_inc(silu_ready, 1)
                for n in range(3):
                    act.wait_ge(wt_made, n + 1)
                    nc.scalar.copy(wt_view(wt_hi, n), wt_psum(n)).then_inc(wt_hi_ready, 1)

                def h_affine(i):
                    act.wait_ge(var_ready, i + 1)
                    nc.scalar.activation(std[:, TPB * i:TPB * i + TPB], var_eps[:, TPB * i:TPB * i + TPB],
                                         ACT.Sqrt).then_inc(std_ready, 1)
                    if i == 0:
                        act.wait_ge(affine_ready, 1)
                    b = i // 2
                    for k in range(EK):
                        act.wait_ge(xt_made, EK * i + k + 1)
                        if i >= 2:
                            act.wait_ge(h_lo_ready, EK * (i - 1))
                        nc.scalar.activation(h_full[:, i % 2, k], ps[:, k, :], ACT.Identity, bias=affine[:, 0, k, b:b + 1],
                                             scale=affine[:, 1, k, b:b + 1]).then_inc(h_full_ready, 1)

                h_affine(0)
                for i in range(BLOCKS):
                    if i + 1 < BLOCKS:
                        h_affine(i + 1)
                    for f in range(4):
                        n = 4 * i + f
                        parts = q_parts if f < 2 else k_parts
                        at = (f % 2) * B * S + i * BLK
                        if n == 0:
                            act.wait_ge(bias_loaded, 9 * DMA)
                        act.wait_ge(qk_made, n + 1)
                        if n >= 2:
                            act.wait_ge(part_m_ready, n - 1)
                        nc.scalar.activation(qk_full[:, n % 2], ps[:, 2 + f, :], ACT.Identity,
                                             bias=bias_qk[:, f // 2, f % 2:f % 2 + 1]).then_inc(qk_full_ready, 1)
                        act.wait_ge(qk_full_ready, n + 1)
                        nc.scalar.copy(parts[:, 0, at:at + BLK], qk_full[:, n % 2]).then_inc(part_h_ready, 1)

            @block.vector
            def _(dve):
                done = [0]

                def link(ins):
                    done[0] += 1
                    ins.then_inc(dve_chain, 1)
                    dve.wait_ge(dve_chain, done[0])

                def layer_norm(i):
                    t0, t1 = TPB * i, TPB * i + TPB
                    dve.wait_ge(x_loaded[i], DMA)
                    for t in range(t0, t1):
                        last = nc.vector.bn_stats(stats[:, t], x_sb[:, t])
                    link(last)
                    for t in range(t0, t1):
                        last = nc.vector.bn_aggr(mean_var[:, t], stats[:, t])
                    link(last)
                    nc.vector.tensor_scalar(var_eps[:, t0:t1], mean_var[:, t0:t1, 1], EPS, None, ALU.add).then_inc(var_ready, 1)
                    dve.wait_ge(std_ready, i + 1)
                    link(nc.vector.reciprocal(rstd0[:, t0:t1], std[:, t0:t1]))
                    link(nc.vector.tensor_tensor(newton[:, t0:t1], rstd0[:, t0:t1], rstd0[:, t0:t1], ALU.mult))
                    link(nc.vector.tensor_tensor(newton[:, t0:t1], newton[:, t0:t1], var_eps[:, t0:t1], ALU.mult))
                    link(nc.vector.tensor_scalar(newton[:, t0:t1], newton[:, t0:t1], -0.5, 1.5, ALU.mult, ALU.add))
                    link(nc.vector.tensor_tensor(rstd[:, t0:t1], rstd0[:, t0:t1], newton[:, t0:t1], ALU.mult))
                    for t in range(t0, t1):
                        last = nc.vector.tensor_scalar(xn[:, t], x_sb[:, t], mean_var[:, t, 0:1], rstd[:, t:t + 1],
                                                       ALU.subtract, ALU.mult)
                    last.then_inc(xn_ready, 1)

                def h_high(i):
                    for k in range(EK):
                        dve.wait_ge(h_full_ready, EK * i + k + 1)
                        if i >= 2:
                            dve.wait_ge(v_made, 2 * (i - 1))
                        nc.vector.tensor_copy(h_hi[:, i % 2, k], h_full[:, i % 2, k]).then_inc(h_hi_ready, 1)

                dve.wait_ge(silu_ready, 1)
                nc.vector.tensor_copy(silu_rep[:, :, :, :],
                                      silu_c[:, :, :].unsqueeze(3).to_broadcast((P, EK, B, P))).then_inc(silu_rep_ready, 1)
                layer_norm(0)
                for n in range(3):
                    dve.wait_ge(wt_hi_ready, n + 1)
                    nc.vector.tensor_tensor(wt_view(wt_lo, n), wt_psum(n), wt_view(wt_hi, n).bitcast(F32),
                                            ALU.subtract).then_inc(wt_ready, 1)
                dve.wait_ge(mod_made, 1)
                mod = ps[:, 3, 0:4 * EK * B].rearrange("p (v k b) -> p v k b", v=4, k=EK)
                link(nc.vector.tensor_copy(affine[:, :, :, :], mod))
                nc.vector.tensor_scalar(affine[:, 1:4:2], affine[:, 1:4:2], 1.0, None, ALU.add).then_inc(affine_ready, 1)
                h_high(0)
                layer_norm(1)
                for i in range(BLOCKS):
                    if i + 1 < BLOCKS:
                        h_high(i + 1)
                    for f in range(4):
                        n = 4 * i + f
                        parts = q_parts if f < 2 else k_parts
                        at = (f % 2) * B * S + i * BLK
                        dve.wait_ge(part_h_ready, n + 1)
                        if n >= 2:
                            dve.wait_ge(part_l_ready, n - 1)
                        link(nc.vector.tensor_tensor(qk_rest[:, n % 2], qk_full[:, n % 2], parts[:, 0, at:at + BLK],
                                                     ALU.subtract))
                        nc.vector.tensor_copy(parts[:, 1, at:at + BLK], qk_rest[:, n % 2]).then_inc(part_m_ready, 1)
                    for half in range(2):
                        n = 2 * i + half
                        dve.wait_ge(v_made, n + 1)
                        if n == 0:
                            dve.wait_ge(bias_loaded, 9 * DMA)
                        t = TPB * i + 2 * half
                        nc.vector.tensor_tensor(
                            v_all[:, :, t:t + 2, :].rearrange("p c t f -> p t c f"),
                            ps[:, 6 + half, :].rearrange("p (t c f) -> p t c f", t=2, c=2),
                            bias_v[:, :].rearrange("p (c f) -> p c f", c=2).unsqueeze(1).to_broadcast((P, 2, 2, P)),
                            ALU.add).then_inc(v_ready, 1)
                    if i + 2 < BLOCKS:
                        layer_norm(i + 2)
                dve.wait_ge(gates_made, 1)
                for b in range(B):
                    link(nc.vector.tensor_scalar(gate_abs[:, b], ps[:, b, :], -1.0, 0.25, ALU.mult, ALU.max))
                    nc.vector.tensor_tensor(gate_abs[:, b], ps[:, b, :], gate_abs[:, b], ALU.max)
                    link(nc.vector.tensor_scalar(gate_sign[:, b], ps[:, b, :], 0.0, 2.0, ALU.is_ge, ALU.mult))
                for b in range(B):
                    nc.vector.scalar_tensor_tensor(
                        out=gates[:, b].rearrange("p g e -> p (g e)"), in0=gate_sign[:, b], scalar=-1.0,
                        in1=gate_abs[:, b], op0=ALU.add, op1=ALU.mult).then_inc(gates_ready, 1)

            @block.tensor
            def _(pe):
                pe.wait_ge(ident_ready, 1)
                pe.wait_ge(w_loaded, 10 * DMA)
                for n, pairs in enumerate(wt_banks):
                    for m, (t, k) in enumerate(pairs):
                        last = nc.tensor.transpose(ps[:, n, m * P:(m + 1) * P], w_rows[:, t, k * P:(k + 1) * P], ident[:, :])
                    last.then_inc(wt_made, 1)
                pe.wait_ge(silu_ready, 1)
                pe.wait_ge(wm_loaded, DMA)
                for v, column in enumerate((0, 1, 3, 4)):
                    for k in range(EK):
                        at = (v * EK + k) * B
                        for kk in range(EK):
                            last = nc.tensor.matmul(ps[:, 3, at:at + B],
                                                    wm[:, kk, column * E + k * P:column * E + (k + 1) * P],
                                                    silu_c[:, kk, :], start=(kk == 0), stop=(kk == EK - 1))
                last.then_inc(mod_made, 1)
                pe.wait_ge(wt_ready, 3)

                def transpose_block(i):
                    pe.wait_ge(xn_ready, i + 1)
                    if i:
                        pe.wait_ge(h_full_ready, EK * i)
                    for k in range(EK):
                        for t in range(TPB):
                            last = nc.tensor.transpose(ps[:, k, t * P:(t + 1) * P], xn[:, TPB * i + t, k * P:(k + 1) * P],
                                                       ident[:, :])
                        last.then_inc(xt_made, 1)

                transpose_block(0)
                pe.wait_ge(affine_ready, 1)
                for i in range(BLOCKS):
                    if i + 1 < BLOCKS:
                        transpose_block(i + 1)
                    pe.wait_ge(h_lo_ready, EK * (i + 1))
                    for f in range(4):
                        if i:
                            pe.wait_ge(qk_full_ready, 4 * (i - 1) + f + 1)
                        for k in range(EK):
                            for a, (w, h) in enumerate(((wt_hi, h_hi), (wt_hi, h_lo), (wt_lo, h_hi))):
                                last = nc.tensor.matmul(ps[:, 2 + f, :], w[:, k, f * P:(f + 1) * P], h[:, i % 2, k],
                                                        start=(k == 0 and a == 0), stop=(k == EK - 1 and a == 2))
                        last.then_inc(qk_made, 1)
                    for half in range(2):
                        if i:
                            pe.wait_ge(v_ready, 2 * (i - 1) + half + 1)
                        for t in range(2):
                            tok = slice((2 * half + t) * P, (2 * half + t + 1) * P)
                            for k in range(EK):
                                for a, (h, w) in enumerate(((h_hi, wt_hi), (h_hi, wt_lo), (h_lo, wt_hi))):
                                    last = nc.tensor.matmul(ps[:, 6 + half, t * E:(t + 1) * E], h[:, i % 2, k, tok],
                                                            w[:, k, 4 * P:6 * P],
                                                            start=(k == 0 and a == 0), stop=(k == EK - 1 and a == 2))
                        last.then_inc(v_made, 1)
                pe.wait_ge(silu_rep_ready, 1)
                pe.wait_ge(h_full_ready, EK * BLOCKS)
                for b in range(B):
                    for g, column in enumerate((2, 5)):
                        for kk in range(EK):
                            last = nc.tensor.matmul(ps[:, b, g * E:(g + 1) * E], silu_rep[:, kk, b, :],
                                                    wm[:, kk, column * E:(column + 1) * E],
                                                    start=(kk == 0), stop=(kk == EK - 1))
                last.then_inc(gates_made, 1)


def attention_and_mlp(nc, scope):
    (sem, x_in, w_proj, b_proj, out, ps, ident, ident_bf, affine, gates, q_parts, k_parts, v_all, windows, phase_sb,
     ramp_sb, spline_w, a_mem, gu_hi, gu_lo, dn_hi, dn_lo, wp_hi, wp_lo, att_hi, att_lo, res, att_dram, den_dram) = names(
        scope, "sem", "x_in", "w_proj", "b_proj", "out", "ps", "ident", "ident_bf", "affine", "gates", "q_parts",
        "k_parts", "v_all", "windows", "phase_sb", "ramp_sb", "spline_w", "a_mem", "gu_hi",
        "gu_lo", "dn_hi", "dn_lo", "wp_hi", "wp_lo", "att_hi", "att_lo", "res", "att_dram", "den_dram")
    with ExitStack() as kept:
        def sb_kept(name, shape, dt=F32):
            return kept.enter_context(nc.sbuf_tensor(name, shape, dt))

        heads = [sb_kept(f"heads{p}", [P, HALVES, BLK]) for p in range(2)]
        wp = sb_kept("wp", [P, EK, E])
        bp = sb_kept("bp", [P, E])
        stats = sb_kept("stats2", [P, TPB, 6])
        mean_var = sb_kept("mean_var2", [P, TPB, 2])
        var_eps = sb_kept("var_eps2", [P, TPB])
        std = sb_kept("std2", [P, TPB])
        rstd0 = sb_kept("rstd02", [P, TPB])
        newton = sb_kept("newton2", [P, TPB])
        rstd = sb_kept("rstd2", [P, TPB])

        def take(start, a, b):
            return a_mem[:, start:start + a * b].rearrange("p (a b) -> p a b", a=a)

        SLAB = EK * BLK
        x_sb = take(0, TILES, E)
        att = take(TILES * E, EK, BLK)
        den = take(TILES * E + SLAB, EK, BLK)
        att_norm = take(TILES * E + 2 * SLAB, EK, BLK)
        xn = take(TILES * E + 3 * SLAB, TPB, E)

        heads_stored = [sem(f"heads_stored{p}") for p in range(2)]
        wp_loaded = sem("wp_loaded")
        bp_loaded = sem("bp_loaded")
        x2_loaded = sem("x2_loaded")
        att_loaded = sem("att_loaded")
        tr_made = sem("tr_made")
        tr_hi = sem("tr_hi")
        tr_lo = sem("tr_lo")
        att_hi_ready = sem("att_hi_ready")
        att_ready = sem("att_ready")
        proj_made = sem("proj_made")
        chain = sem("mlp_chain")
        var_ready = sem("var_ready2")
        std_ready = sem("std_ready2")
        xn_ready = sem("xn_ready2")
        xt_made = sem("xt_made2")
        h_full_ready = sem("h_full_ready2")
        h_hi_ready = sem("h_hi_ready2")
        h_ready = sem("h_ready2")
        gu_made = sem("gu_made")
        silu_ready = sem("silu_ready2")
        inter_ready = sem("inter_ready")
        in_hi_ready = sem("in_hi_ready")
        in_ready = sem("in_ready")
        down_made = sem("down_made")
        down_read = sem("down_read")
        y_ready = sem("y_ready")
        y_stored = sem("y_stored")

        G_BANK, D_BANK, X_BANK = 0, 4, 6
        PROJECT_AT = 1
        TR = 3 * PIECES // 4 + 1
        T_RING = 3
        FIRST_PROJECT = STEPS - 3
        FIRST_HEADS = 6
        prod = lambda a, b: ((a[0], b[0]), (a[0], b[1]), (a[1], b[0]))

        def tr_out(n, w):
            if n == 0:
                return w[2][:, :, :].rearrange("p k (r e) -> p r k e", r=2)
            n -= 1
            weight, m = n // 4, 4 * (n % 4)
            if weight < 2:
                return w[0][:, weight, :, m * 64:(m + 4) * 64].rearrange("p k i -> p i k")
            return w[1][:, :, m * 16:(m + 4) * 16].rearrange("p i o -> p o i")

        def tr_in(n):
            bank = ps[:, n % T_RING, :]
            if n == 0:
                return bank.rearrange("p (r k e) -> p r k e", r=2, k=EK)
            if (n - 1) // 4 < 2:
                return bank.rearrange("p (i k) -> p i k", k=EK)
            return bank.rearrange("p (o i) -> p o i", i=IK)

        def load_att(i, b, half):
            for c in range(EK):
                part = b + 2 * c
                nc.sync.dma_start(att[:, c, :], att_dram[bass.ds(part, 1), :, bass.ds(half * BLK, BLK)])\
                  .then_inc(att_loaded, DMA)
                for g in range(2 * GH):
                    nc.sync.dma_start(den[HD * g:HD * g + HD, c, :],
                                 den_dram[bass.ds(part, 1), g, bass.ds(half * BLK, BLK)]
                                 .rearrange("o s -> (o s)").partition_broadcast(HD)).then_inc(att_loaded, DMA)

        def project(i, bank=X_BANK):
            nc.tensor.wait_ge(att_ready, (i + 1) * EK)
            for half in range(2):
                for t in range(2):
                    tok = slice((2 * half + t) * P, (2 * half + t + 1) * P)
                    for k in range(EK):
                        for a, (x, w) in enumerate(prod((att_hi, att_lo), (wp_hi, wp_lo))):
                            last = nc.tensor.matmul(ps[:, bank + half, t * E:(t + 1) * E], x[:, k, tok], w[:, k, :],
                                                    start=(k == 0 and a == 0), stop=(k == EK - 1 and a == 2))
                last.then_inc(proj_made, 1)

        done = [0]

        def link(ins):
            done[0] += 1
            ins.then_inc(chain, 1)
            nc.vector.wait_ge(chain, done[0])

        def att_reciprocal(i, c):
            nc.vector.wait_ge(att_loaded, (i + 1) * (EK * (2 * GH + 1) * DMA))
            link(nc.vector.reciprocal(den[:, c], den[:, c]))

        def att_high(i, c):
            if i:
                nc.vector.wait_ge(att_ready, EK * i)
            link(nc.vector.tensor_tensor(att_norm[:, c], att[:, c], den[:, c], ALU.mult))
            if i:
                nc.vector.wait_ge(proj_made, 2 * i)
            nc.vector.tensor_copy(att_hi[:, c], att_norm[:, c]).then_inc(att_hi_ready, 1)

        def project_gated(i, b, half, bank=X_BANK):
            nc.vector.wait_ge(proj_made, 2 * i + half + 1)
            part = res[:, 2 * half:2 * half + 2, :]
            link(nc.vector.tensor_tensor(part, ps[:, bank + half, :].rearrange("p (t e) -> p t e", t=2),
                                         bp[:, :].unsqueeze(1).to_broadcast((P, 2, E)), ALU.add))
            link(nc.vector.tensor_tensor(part, part, gates[:, b, 0, :].unsqueeze(1).to_broadcast((P, 2, E)),
                                         ALU.mult))

        def residual(i, half):
            x = x_sb[:, TPB * i + 2 * half:TPB * i + 2 * half + 2, :]
            link(nc.vector.tensor_tensor(x, x, res[:, 2 * half:2 * half + 2, :], ALU.add))
            for t in range(2 * half, 2 * half + 2):
                last = nc.vector.bn_stats(stats[:, t], x_sb[:, TPB * i + t])
            link(last)

        def variance():
            for t in range(TPB):
                last = nc.vector.bn_aggr(mean_var[:, t], stats[:, t])
            link(last)
            nc.vector.tensor_scalar(var_eps[:, :], mean_var[:, :, 1], EPS, None, ALU.add).then_inc(var_ready, 1)

        def normalise(i):
            nc.vector.wait_ge(std_ready, i + 1)
            link(nc.vector.reciprocal(rstd0[:, :], std[:, :]))
            link(nc.vector.tensor_tensor(newton[:, :], rstd0[:, :], rstd0[:, :], ALU.mult))
            link(nc.vector.tensor_tensor(newton[:, :], newton[:, :], var_eps[:, :], ALU.mult))
            link(nc.vector.tensor_scalar(newton[:, :], newton[:, :], -0.5, 1.5, ALU.mult, ALU.add))
            link(nc.vector.tensor_tensor(rstd[:, :], rstd0[:, :], newton[:, :], ALU.mult))
            for t in range(TPB):
                last = nc.vector.tensor_scalar(xn[:, t], x_sb[:, TPB * i + t], mean_var[:, t, 0:1], rstd[:, t:t + 1],
                                               ALU.subtract, ALU.mult)
            last.then_inc(xn_ready, 1)

        def root(i):
            nc.scalar.wait_ge(var_ready, i + 1)
            nc.scalar.activation(std[:, :], var_eps[:, :], ACT.Sqrt).then_inc(std_ready, 1)

        def att_low(i, chunks=range(EK)):
            for c in chunks:
                nc.gpsimd.wait_ge(att_hi_ready, EK * i + c + 1)
                nc.gpsimd.tensor_tensor(att_lo[:, c], att_norm[:, c], att_hi[:, c].bitcast(F32), ALU.subtract)\
                  .then_inc(att_ready, 1)

        with ExitStack() as mem:
            def sb(name, shape, dt=F32):
                return mem.enter_context(nc.sbuf_tensor(name, shape, dt))

            qa, ka = ([a_mem[0:KROWS, (2 * n + p) * GH * S // 2:(2 * n + p + 1) * GH * S // 2].bitcast(BF16)
                       .rearrange("r (j s) -> r j s", j=GH) for p in range(2)] for n in range(2))
            qb = [sb(f"qb{p}", [KROWS + MROWS, GH, S], BF16) for p in range(2)]
            kb = [sb(f"kb{p}", [KROWS + MROWS, GH, S], BF16) for p in range(2)]
            vg = [sb(f"vg{p}", [P, KT, GH, 2 * HD]) for p in range(2)]
            probs = sb("probs", [P, 2, GH, BLK])
            max_parts = sb("max_parts", [P, GH * KT, HALVES])
            neg_max = sb("neg_max", [P, GH * KT])
            rest = sb("rest", [P, 2, GH * KT])
            neg_split = sb("neg_split", [P, MROWS, GH * KT], BF16)
            neg_rows = sb("neg_rows", [MROWS * GH * KT, P], BF16)
            coef = sb("coef", [P, 6, 3, PIECES])
            diff = sb("diff", [P, 3, PIECES, 10])
            z = sb("z", [P, 4, P])
            y = sb("y", [P, 4, P])
            bend = sb("bend", [P, 4, P])

            a_loaded = [sem(f"a_loaded{p}") for p in range(2)]
            b_loaded = [sem(f"b_loaded{p}") for p in range(2)]
            v_loaded = [sem(f"v_loaded{p}") for p in range(2)]
            max_loaded = [sem(f"max_loaded{p}") for p in range(2)]
            ones_ready = sem("ones_ready")
            a_full = sem("a_full")
            a_free = sem("a_free")
            neg_ready = sem("neg_ready")
            max_chain = sem("max_chain")
            b_full = sem("b_full")
            p_ready = sem("p_ready")
            pv_done = sem("pv_done")
            heads_ready = sem("heads_ready")
            spline_chain = sem("spline_chain")
            spline_ready = sem("spline_ready")

            SLOTS = len(Q_SLOTS)
            A_BANK, B_BANK, O_BANK = 0, RING, 2 * RING
            v_view = v_all[:, :, :, :].rearrange("p c (b k) (g j d) -> p (c b) k g (j d)", b=B, g=2, j=GH)
            neg_psum = ps[:, A_BANK + A_UNITS % RING, :].bitcast(BF16)[0:MROWS * GH * KT, 0:P]

            with nc.Block() as block:

                @block.sync
                def _(sp):
                    def load_stack(q_to, k_to, at, p, loaded):
                        for to, parts, slots in ((q_to, q_parts, Q_SLOTS), (k_to, k_parts, K_SLOTS)):
                            for r, part in enumerate(slots):
                                sp.dma_start(to[HD * r:HD * r + HD], parts[64 * p:64 * p + 64, part, bass.ds(at, S)])\
                                  .then_inc(loaded, DMA)

                    def load_b(it, at, p):
                        load_stack(qb[p], kb[p], at, p, b_loaded[p])
                        for kt in range(KT):
                            sp.dma_start(vg[p][:, kt, :, 0:HD],
                                         v_view[:, bass.ds(it, 1), kt, p, :].rearrange("p o (j d) -> p (o j) d", j=GH))\
                              .then_inc(v_loaded[p], DMA)

                    def load_max(p):
                        sp.dma_start(qb[p][KROWS:KROWS + MROWS], neg_rows[:, :]).then_inc(max_loaded[p], DMA)

                    def store_heads(it, p):
                        for j in range(GH):
                            at = 64 * p + HD * j
                            sp.dma_start(att_dram[bass.ds(it, 1), at:at + HD, :], heads[p][32 * j:32 * j + HD])\
                              .then_inc(heads_stored[p], DMA)
                            sp.dma_start(den_dram[bass.ds(it, 1), GH * p + j:GH * p + j + 1, :],
                                         heads[p][32 * j + HD:32 * j + HD + 1]).then_inc(heads_stored[p], DMA)

                    def in_register(value, most=1 << 16):
                        return sp.snap(sp.to_reg(value), min_val=0, max_val=most)

                    def pair(it, number, last):
                        this, this_at = number(it, 2), number(it * S, 2 * S)
                        after, after_at = (None, None) if last else (number(it + 1, 3), number((it + 1) * S, 3 * S))
                        a_issued = [number((it * 2 + p + 1) * A_ALL) for p in range(2)]
                        pv_issued = [number((it * 2 + p) * STEPS + START) for p in range(2)]
                        a_read = [number((it * 2 + p + 2) * A_ALL) for p in range(2)]
                        heads_read = [number((it * 2 + p + 1) * HALVES + START) for p in range(2)]
                        for p in range(2):
                            sp.wait_ge(a_full, a_issued[p])
                            if not last:
                                load_stack(qa[p], ka[p], after_at, p, a_loaded[p])
                            if not last or p == 0:
                                sp.wait_ge(pv_done, pv_issued[p])
                                load_b(after if p else this, after_at if p else this_at, 1 - p)
                                sp.wait_ge(a_free, a_read[p])
                                load_max(1 - p)
                            if last and p:
                                for parity in range(2):
                                    sp.wait_ge(heads_stored[parity], 3 * 2 * GH * DMA + DMA)
                                load_att(0, 0, 0)
                                sp.dma_start(x_sb, x_in.rearrange("(t p) e -> p t e", p=P)).then_inc(x2_loaded, DMA)
                                sp.wait_ge(att_ready, EK)
                                load_att(1, 0, 1)
                            sp.wait_ge(heads_ready, heads_read[p])
                            store_heads(this, p)

                    for p in range(2):
                        sp.sem_inc(heads_stored[p], DMA)
                    load_stack(qa[0], ka[0], 0, 0, a_loaded[0])
                    load_b(0, 0, 0)
                    load_stack(qa[1], ka[1], 0, 1, a_loaded[1])
                    sp.dma_start(wp[:, :, :], w_proj.rearrange("(r p) e -> p r e", p=P)).then_inc(wp_loaded, DMA)
                    sp.dma_start(bp[:, :], b_proj.partition_broadcast(P)).then_inc(bp_loaded, DMA)
                    sp.wait_ge(a_free, A_ALL)
                    load_max(0)
                    with sp.Fori(0, GROUPS // 2 - 1) as it:
                        pair(it, in_register, False)
                    pair(GROUPS // 2 - 1, lambda value, most=0: value, True)

                @block.tensor
                def _(pe):
                    def a_unit(it, p, u):
                        g = it * 2 + p
                        j, t, half = u // (KT * HALVES), u // HALVES % KT, u % HALVES
                        if u == 0:
                            pe.wait_ge(a_loaded[p], (it + 1) * (2 * SLOTS * DMA))
                        if u < 2 and not (isinstance(g, int) and g == 0):
                            pe.wait_ge(a_free, g * A_ALL + (u - 1))
                        if u >= RING:
                            pe.wait_ge(a_free, g * A_ALL + (u - RING + 1))
                        nc.tensor.matmul(ps[:, A_BANK + u % RING, :], qa[p][:, j, t * P:(t + 1) * P],
                                         ka[p][:, j, half * BLK:(half + 1) * BLK], start=True, stop=True).then_inc(a_full, 1)

                    def max_transpose(it, p):
                        pe.wait_ge(neg_ready, it * 2 + (p + 1))
                        nc.tensor.transpose(neg_psum, neg_split[:, :, :].rearrange("p m u -> p (m u)"), ident_bf[:, :])\
                          .then_inc(a_full, 1)

                    def b_unit(it, p, n, j):
                        g = it * 2 + p
                        u, kt, half = GH * n + j, n // HALVES, n % HALVES
                        if u == 0:
                            pe.wait_ge(b_loaded[p], (it + 1) * (2 * SLOTS * DMA))
                            pe.wait_ge(max_loaded[p], (it + 1) * DMA)
                        if u >= RING:
                            pe.wait_ge(p_ready, g * B_UNITS + (u - RING + 1))
                        nc.tensor.matmul(ps[:, B_BANK + u % RING, :], kb[p][:, j, kt * P:(kt + 1) * P],
                                         qb[p][:, j, half * BLK:(half + 1) * BLK], start=True, stop=True).then_inc(b_full, 1)

                    def pv(it, p, n):
                        g = it * 2 + p
                        kt, half = n // HALVES, n % HALVES
                        if n == 0:
                            pe.wait_ge(v_loaded[p], (it + 1) * (KT * DMA))
                            pe.wait_ge(heads_ready, g * HALVES + START)
                        pe.wait_ge(p_ready, g * B_UNITS + GH * (n + 1))
                        for j in range(GH):
                            last = nc.tensor.matmul(ps[32 * j:32 * j + 32, O_BANK + half, :], vg[p][:, kt, j, :],
                                                    probs[:, n % 2, j, :], start=(kt == 0), stop=(kt == KT - 1))
                        last.then_inc(pv_done, 1)

                    def weight_transpose(n, m):
                        if n == 0 and m == 0:
                            pe.wait_ge(wp_loaded, DMA)
                            pe.wait_ge(spline_ready, 1)
                            pe.wait_ge(a_free, GROUPS * A_ALL)
                        if n >= T_RING and m == 0:
                            pe.wait_ge(tr_lo, n - T_RING + 1)
                        if n == 0:
                            src = wp[:, m // 2, (m % 2) * P:(m % 2 + 1) * P]
                        else:
                            src = spline_w[:, (n - 1) // 4, 4 * ((n - 1) % 4) + m, :]
                        made = nc.tensor.transpose(ps[:, n % T_RING, m * P:(m + 1) * P], src, ident[:, :])
                        if m == 3:
                            made.then_inc(tr_made, 1)

                    def group(it, p, after_next=True):
                        it_a, p_a = it + p, 1 - p
                        u = A_AHEAD
                        for n in range(STEPS):
                            for j in range(GH):
                                b_unit(it, p, n, j)
                                if n < len(A_PER_STEP):
                                    for _ in range(A_PER_STEP[n] * (j + 1) // GH - A_PER_STEP[n] * j // GH):
                                        a_unit(it_a, p_a, u)
                                        u += 1
                                elif n == STEPS - 1 and after_next:
                                    a_unit(it + 1, p, j)
                            if n:
                                pv(it, p, n - 1)
                            if n == STEPS - 2:
                                max_transpose(it_a, p_a)
                        pv(it, p, STEPS - 1)

                    def last_group(it, p):
                        for n in range(STEPS):
                            for j in range(GH):
                                b_unit(it, p, n, j)
                                if n < TR:
                                    weight_transpose(n, j)
                            if n:
                                pv(it, p, n - 1)
                            if n == FIRST_PROJECT:
                                pe.wait_ge(tr_lo, TR)
                                project(0, A_BANK)
                        pv(it, p, STEPS - 1)

                    pe.sem_inc(pv_done, START)
                    pe.wait_ge(ones_ready, 4)
                    for u in range(A_UNITS):
                        a_unit(0, 0, u)
                    max_transpose(0, 0)
                    for u in range(A_AHEAD):
                        a_unit(0, 1, u)
                    with pe.Fori(0, GROUPS // 2 - 1) as it:
                        group(it, 0)
                        group(it, 1)
                    group(GROUPS // 2 - 1, 0, after_next=False)
                    last_group(GROUPS // 2 - 1, 1)

                @block.vector
                def _(dve):
                    CHAIN = 5

                    def maxima(g):
                        for u in range(A_UNITS):
                            dve.wait_ge(a_full, g * A_ALL + (u + 1))
                            nc.vector.tensor_reduce(max_parts[:, u // HALVES, u % HALVES:u % HALVES + 1],
                                                    ps[:, A_BANK + u % RING, :], AX, ALU.max).then_inc(a_free, 1)
                        done = [0]

                        def link(ins):
                            done[0] += 1
                            ins.then_inc(max_chain, 1)
                            dve.wait_ge(max_chain, g * CHAIN + done[0])

                        dve.wait_ge(a_free, g * A_ALL + A_UNITS)
                        link(nc.vector.tensor_reduce(neg_max[:, :], max_parts[:, :, :], AX, ALU.max, negate=True))
                        link(nc.vector.tensor_copy(neg_split[:, 0], neg_max[:, :]))
                        link(nc.vector.tensor_tensor(rest[:, 0], neg_max[:, :], neg_split[:, 0], ALU.subtract))
                        link(nc.vector.tensor_copy(neg_split[:, 1], rest[:, 0]))
                        link(nc.vector.tensor_tensor(rest[:, 1], rest[:, 0], neg_split[:, 1], ALU.subtract))
                        assert done[0] == CHAIN
                        nc.vector.tensor_copy(neg_split[:, 2], rest[:, 1]).then_inc(neg_ready, 1)
                        dve.wait_ge(a_full, (g + 1) * A_ALL)
                        nc.vector.tensor_copy(neg_rows[:, :], neg_psum).then_inc(a_free, 1)

                    for p in range(2):
                        nc.vector.memset(vg[p][:, :, :, HD:2 * HD], 1.0).then_inc(ones_ready, 1)
                    for p in range(2):
                        nc.vector.memset(kb[p][KROWS:KROWS + MROWS], 1.0).then_inc(ones_ready, 1)
                    maxima(0)
                    with dve.Fori(0, GROUPS // 2 - 1) as it:
                        maxima(it * 2 + 1)
                        maxima(it * 2 + 2)
                    maxima(GROUPS - 1)
                    dve.sem_inc(down_read, START)
                    dve.wait_ge(b_loaded[1], GROUPS // 2 * 2 * SLOTS * DMA)
                    dve.wait_ge(v_loaded[1], GROUPS // 2 * KT * DMA)
                    for n in range(TR):
                        dve.wait_ge(tr_made, n + 1)
                        nc.vector.tensor_copy(tr_out(n, (gu_hi, dn_hi, wp_hi)), tr_in(n)).then_inc(tr_hi, 1)
                        dve.wait_ge(tr_hi, n + 1)
                        nc.vector.tensor_tensor(tr_out(n, (gu_lo, dn_lo, wp_lo)), tr_in(n),
                                                tr_out(n, (gu_hi, dn_hi, wp_hi)).bitcast(F32), ALU.subtract).then_inc(tr_lo, 1)
                        if FIRST_HEADS <= n < FIRST_HEADS + 2 * EK:
                            (att_high if (n - FIRST_HEADS) % 2 else att_reciprocal)(0, (n - FIRST_HEADS) // 2)
                    dve.wait_ge(bp_loaded, DMA)
                    dve.wait_ge(x2_loaded, DMA)
                    for half in range(2):
                        project_gated(0, 0, half, A_BANK)
                        residual(0, half)
                    variance()
                    att_reciprocal(1, 0)
                    normalise(0)

                @block.scalar
                def _(act):
                    def exponentials(it, p):
                        g = it * 2 + p
                        for u in range(B_UNITS):
                            n, j = u // GH, u % GH
                            act.wait_ge(b_full, g * B_UNITS + (u + 1))
                            if u == 0:
                                act.wait_ge(pv_done, g * STEPS + START)
                            if j == 0 and n >= 2:
                                act.wait_ge(pv_done, g * STEPS + (n - 1 + START))
                            nc.scalar.activation(probs[:, n % 2, j, :], ps[:, B_BANK + u % RING, :], ACT.Exp,
                                                 scale=SCALE).then_inc(p_ready, 1)

                    def copy_heads(it, p):
                        g = it * 2 + p
                        for half in range(HALVES):
                            act.wait_ge(pv_done, g * STEPS + (STEPS - HALVES + half + 1 + START))
                            if half == 0:
                                act.wait_ge(heads_stored[p], it * (2 * GH * DMA) + DMA)
                            nc.scalar.copy(heads[p][:, half, :], ps[:, O_BANK + half, :]).then_inc(heads_ready, 1)

                    act.preload_act_table(ACT.Exp)
                    act.sem_inc(heads_ready, START)
                    with act.Fori(0, GROUPS // 2 - 1) as it:
                        for p in range(2):
                            exponentials(it, p)
                            copy_heads(it, p)
                    exponentials(GROUPS // 2 - 1, 0)
                    copy_heads(GROUPS // 2 - 1, 0)
                    exponentials(GROUPS // 2 - 1, 1)
                    root(0)
                    copy_heads(GROUPS // 2 - 1, 1)

                @block.gpsimd
                def _(pool):
                    done = [0]

                    def link(ins):
                        done[0] += 1
                        ins.then_inc(spline_chain, 1)
                        pool.wait_ge(spline_chain, done[0])

                    def tt(to, a, b, op):
                        link(nc.gpsimd.tensor_tensor(to, a, b, op))

                    pts, half_pts = windows[:, :, :, :], diff[:, :, :, 0:5]
                    link(nc.gpsimd.tensor_scalar(half_pts, pts, 0.5, None, ALU.mult))
                    d1, d2, d3 = diff[:, :, :, 5:9], diff[:, :, :, 0:3], diff[:, :, :, 3:5]
                    tt(d1, diff[:, :, :, 1:5], diff[:, :, :, 0:4], ALU.subtract)
                    tt(d2, d1[:, :, :, 1:4], d1[:, :, :, 0:3], ALU.subtract)
                    tt(d3, d2[:, :, :, 1:3], d2[:, :, :, 0:2], ALU.subtract)
                    c0 = windows[:, :, :, 1]
                    c1, c2, c3, e2, e3 = (coef[:, n] for n in range(5))
                    tt(c1, d1[:, :, :, 0], d1[:, :, :, 1], ALU.add)
                    tt(c2, d2[:, :, :, 0], d3[:, :, :, 0], ALU.subtract)
                    link(nc.gpsimd.tensor_copy(c3, d3[:, :, :, 0]))
                    tt(e2, d3[:, :, :, 0], d3[:, :, :, 1], ALU.add)
                    tt(e3, d3[:, :, :, 1], d3[:, :, :, 0], ALU.subtract)
                    for q in range(PIECES // 4):
                        m = slice(4 * q, 4 * q + 4)

                        def wide(a):
                            return a.unsqueeze(2).to_broadcast((P, 4, P))

                        tt(z[:, :, :], ramp_sb[:, :].unsqueeze(1).to_broadcast((P, 4, P)), wide(phase_sb[:, m]), ALU.add)
                        link(nc.gpsimd.tensor_scalar(y[:, :, :], z[:, :, :], -1.0, None, ALU.add))
                        link(nc.gpsimd.tensor_scalar(y[:, :, :], y[:, :, :], 0.0, None, ALU.max))
                        for n in range(3):
                            w = spline_w[:, n, m, :]
                            tt(w, z[:, :, :], wide(c3[:, n, m]), ALU.mult)
                            tt(w, w, wide(c2[:, n, m]), ALU.add)
                            tt(w, w, z[:, :, :], ALU.mult)
                            tt(w, w, wide(c1[:, n, m]), ALU.add)
                            tt(w, w, z[:, :, :], ALU.mult)
                            tt(w, w, wide(c0[:, n, m]), ALU.add)
                            tt(bend[:, :, :], y[:, :, :], wide(e3[:, n, m]), ALU.mult)
                            tt(bend[:, :, :], bend[:, :, :], wide(e2[:, n, m]), ALU.subtract)
                            tt(bend[:, :, :], bend[:, :, :], y[:, :, :], ALU.mult)
                            tt(bend[:, :, :], bend[:, :, :], y[:, :, :], ALU.mult)
                            tt(w, w, bend[:, :, :], ALU.add)
                    pool.sem_inc(spline_ready, 1)
                    att_low(0)

        with ExitStack() as mem:
            def sb(name, shape, dt=F32):
                return mem.enter_context(nc.sbuf_tensor(name, shape, dt))

            h_full = sb("h_full2", [P, EK, BLK])
            h_hi = sb("h_hi2", [P, EK, BLK], F32R)
            h_lo = sb("h_lo2", [P, EK, BLK], F32R)
            silu = sb("silu", [P, 2, BLK])
            inter = sb("inter", [P, 2, BLK])
            in_hi = sb("in_hi", [P, IK, BLK], F32R)
            in_lo = sb("in_lo", [P, IK, BLK], F32R)
            ffn = sb("ffn", [P, TPB, E])
            y_sb = sb("y_sb", [P, TPB, E])


            with nc.Block() as block:

                @block.sync
                def _(sp):
                    def store(i):
                        sp.wait_ge(y_ready, i * 2 + 2)
                        sp.dma_start(out[bass.ds(i * BLK, BLK), :].rearrange("(t p) e -> p t e", p=P), y_sb[:, :, :])\
                          .then_inc(y_stored, DMA)

                    for p in range(2):
                        sp.wait_ge(heads_stored[p], GROUPS // 2 * 2 * GH * DMA + DMA)
                    for i in range(BLOCKS):
                        if i + 2 < BLOCKS:
                            sp.wait_ge(att_ready, EK * (i + 2))
                            load_att(i + 2, (i + 2) // 2, (i + 2) % 2)
                        store(i)
                    sp.wait_ge(y_stored, BLOCKS * DMA)

                @block.tensor
                def _(pe):
                    def transpose_block(i):
                        pe.wait_ge(xn_ready, i + 1)
                        for k in range(EK):
                            for t in range(TPB):
                                last = nc.tensor.transpose(ps[:, X_BANK + k, t * P:(t + 1) * P], xn[:, t, k * P:(k + 1) * P],
                                                           ident[:, :])
                            last.then_inc(xt_made, 1)

                    def gate_up(i, chunks):
                        for c in chunks:
                            if c == 0:
                                pe.wait_ge(h_ready, (i + 1) * EK)
                            if c >= 2:
                                pe.wait_ge(inter_ready, i * IK + (c - 1))
                            for g in range(2):
                                for k in range(EK):
                                    for a, (w, x) in enumerate(prod((gu_hi, gu_lo), (h_hi, h_lo))):
                                        last = nc.tensor.matmul(ps[:, G_BANK + 2 * (c % 2) + g, :],
                                                                w[:, g, k, c * P:(c + 1) * P], x[:, k, :],
                                                                start=(k == 0 and a == 0), stop=(k == EK - 1 and a == 2))
                            last.then_inc(gu_made, 1)

                    def down(i, half):
                        pe.wait_ge(down_read, i * 2 + START)
                        for t in range(2):
                            tok = slice((2 * half + t) * P, (2 * half + t + 1) * P)
                            for c in range(IK):
                                if half == 0 and t == 0 and c >= IK - 2:
                                    pe.wait_ge(in_ready, i * IK + (c + 1))
                                elif half == 0 and t == 0 and c == 0:
                                    pe.wait_ge(in_ready, i * IK + (IK - 2))
                                for a, (x, w) in enumerate(prod((in_hi, in_lo), (dn_hi, dn_lo))):
                                    last = nc.tensor.matmul(ps[:, D_BANK + half, t * E:(t + 1) * E], x[:, c, tok], w[:, c, :],
                                                            start=(c == 0 and a == 0), stop=(c == IK - 1 and a == 2))
                        last.then_inc(down_made, 1)

                    transpose_block(0)
                    with pe.Fori(0, BLOCKS - 1) as i:
                        gate_up(i, range(PROJECT_AT))
                        project(i + 1)
                        gate_up(i, range(PROJECT_AT, IK))
                        transpose_block(i + 1)
                        down(i, 0)
                        down(i, 1)
                    gate_up(BLOCKS - 1, range(IK))
                    down(BLOCKS - 1, 0)
                    down(BLOCKS - 1, 1)

                @block.scalar
                def _(act):
                    def h_affine(i, b):
                        for k in range(EK):
                            act.wait_ge(xt_made, i * EK + (k + 1))
                            nc.scalar.activation(h_full[:, k], ps[:, X_BANK + k, :], ACT.Identity,
                                                 bias=affine[:, 2, k, b:b + 1], scale=affine[:, 3, k, b:b + 1])\
                              .then_inc(h_full_ready, 1)

                    h_affine(0, 0)
                    for i in range(BLOCKS):
                        for c in range(IK):
                            n = i * IK + c
                            act.wait_ge(gu_made, n + 1)
                            if n >= 2:
                                act.wait_ge(inter_ready, n - 1)
                            nc.scalar.activation(silu[:, c % 2], ps[:, G_BANK + 2 * (c % 2), :], ACT.Silu).then_inc(silu_ready, 1)
                            act.wait_ge(inter_ready, n + 1)
                            nc.scalar.copy(in_hi[:, c], inter[:, c % 2]).then_inc(in_hi_ready, 1)
                            if c == PROJECT_AT + 3 and i + 1 < BLOCKS:
                                root(i + 1)
                        if i + 1 < BLOCKS:
                            h_affine(i + 1, (i + 1) // 2)

                @block.gpsimd
                def _(pool):
                    def h_low(i):
                        for k in range(EK):
                            pool.wait_ge(h_hi_ready, EK * i + k + 1)
                            nc.gpsimd.tensor_tensor(h_lo[:, k], h_full[:, k], h_hi[:, k].bitcast(F32), ALU.subtract)\
                              .then_inc(h_ready, 1)

                    h_low(0)
                    att_low(1)
                    for i in range(BLOCKS):
                        for c in range(IK):
                            n = i * IK + c
                            pool.wait_ge(in_hi_ready, n + 1)
                            nc.gpsimd.tensor_tensor(in_lo[:, c], inter[:, c % 2], in_hi[:, c].bitcast(F32), ALU.subtract)\
                              .then_inc(in_ready, 1)
                        if i + 1 < BLOCKS:
                            h_low(i + 1)
                        for half in range(2):
                            if i + 2 < BLOCKS:
                                att_low(i + 2, [half])
                            pool.wait_ge(down_read, 2 * i + half + 1 + START)
                            if i and half == 0:
                                pool.wait_ge(y_stored, i * DMA)
                            nc.gpsimd.tensor_tensor(y_sb[:, 2 * half:2 * half + 2, :], ffn[:, 2 * half:2 * half + 2, :],
                                                    x_sb[:, TPB * i + 2 * half:TPB * i + 2 * half + 2, :], ALU.add)\
                                .then_inc(y_ready, 1)

                @block.vector
                def _(dve):
                    def h_high(i):
                        for k in range(EK):
                            dve.wait_ge(h_full_ready, i * EK + k + 1)
                            nc.vector.tensor_copy(h_hi[:, k], h_full[:, k]).then_inc(h_hi_ready, 1)

                    h_high(0)
                    att_high(1, 0)
                    att_reciprocal(1, 1)
                    att_high(1, 1)
                    for i in range(BLOCKS):
                        for c in range(IK):
                            n = i * IK + c
                            dve.wait_ge(silu_ready, n + 1)
                            if n >= 2:
                                dve.wait_ge(in_ready, n - 1)
                            nc.vector.tensor_tensor(inter[:, c % 2], silu[:, c % 2], ps[:, G_BANK + 2 * (c % 2) + 1, :],
                                                    ALU.mult).then_inc(inter_ready, 1)
                            if i + 1 < BLOCKS:
                                if c in (PROJECT_AT, PROJECT_AT + 2):
                                    project_gated(i + 1, (i + 1) // 2, (c - PROJECT_AT) // 2)
                                elif c in (PROJECT_AT + 1, PROJECT_AT + 3):
                                    residual(i + 1, (c - PROJECT_AT) // 2)
                                    if c == PROJECT_AT + 3:
                                        variance()
                                        normalise(i + 1)
                        if i + 1 < BLOCKS:
                            h_high(i + 1)
                        for half in range(2):
                            if i + 2 < BLOCKS:
                                att_reciprocal(i + 2, half)
                                att_high(i + 2, half)
                            dve.wait_ge(down_made, 2 * i + half + 1)
                            if i:
                                dve.wait_ge(y_ready, 2 * (i - 1) + half + 1)
                            nc.vector.tensor_tensor(ffn[:, 2 * half:2 * half + 2, :],
                                                    ps[:, D_BANK + half, :].rearrange("p (t e) -> p t e", t=2),
                                                    gates[:, i // 2, 1, :].unsqueeze(1).to_broadcast((P, 2, E)), ALU.mult)\
                                .then_inc(down_read, 1)


def _spline_grid(np):
    step = (N_CTRL - 1) / (INTER * E - 1)
    column, partition = np.meshgrid(np.arange(PIECES), np.arange(P))
    t = (P * (P * column + partition)) * step
    first = np.floor(t).astype(np.int64)
    assert (first == (P - 1) * column + np.maximum(partition - 1, 0)).all()
    return (t - first).astype(np.float32), (np.arange(P) * step).astype(np.float32)


def kernel(**inputs):
    import numpy as np
    import concourse.bacc as bacc
    from concourse.bass_utils import run_bass_kernel_spmd

    def ends_repeated(cp):
        cp = np.asarray(cp)
        return np.concatenate([cp[:1], cp, cp[-1:], cp[-1:]])

    phase, ramp = _spline_grid(np)
    arrays = {
        "x_in": np.ascontiguousarray(inputs["L0_attn_query"]).reshape(B * S, E),
        "w_qkv": np.ascontiguousarray(inputs["L0_attn_Wqkv"]),
        "b_qkv": np.ascontiguousarray(inputs["L0_attn_bqkv"]),
        "w_proj": np.ascontiguousarray(inputs["L0_attn_Wproj"]),
        "b_proj": np.ascontiguousarray(inputs["L0_attn_bproj"]),
        "gate_cp": ends_repeated(inputs["L0_ffn_gate_cp"]),
        "up_cp": ends_repeated(inputs["L0_ffn_up_cp"]),
        "down_cp": ends_repeated(inputs["L0_ffn_down_cp"]),
        "c_in": np.ascontiguousarray(inputs["L0_c"]),
        "w_mod": np.ascontiguousarray(inputs["L0_wmod"]),
        "phase": phase,
        "ramp": ramp,
    }
    nc = bacc.Bacc("TRN2", target_bir_lowering=False, num_devices=1)
    args = [nc.dram_tensor(name, a.shape, mybir.dt.from_np(a.dtype), kind="ExternalInput").ap()
            for name, a in arrays.items()]
    out = nc.dram_tensor("out", [B * S, E], F32, kind="ExternalOutput").ap()
    adaln_block(nc, *args, out)
    result = run_bass_kernel_spmd(nc, [arrays], core_ids=[0])
    return result.results[0]["out"].reshape(B, S, E)
```

```python
import concourse.bass as bass
from concourse import mybir
from concourse.alu_op_type import AluOpType as ALU
from contextlib import ExitStack

F32 = mybir.dt.float32
F32R = mybir.dt.float32r
BF16 = mybir.dt.bfloat16
I32 = mybir.dt.int32
ACT = mybir.ActivationFunctionType
AX = mybir.AxisListType.X

P = 128
B, S, E = 2, 1024, 256
H, HD = 16, 16
INTER = 1024
EK = E // P
IK = INTER // P
TILES = B * S // P
BLK = 512
BLOCKS = B * S // BLK
TPB = BLK // P
KT = S // P
GH = 4
GROUPS = B * H // GH
HALVES = S // BLK
STEPS = KT * HALVES
A_UNITS = GH * KT * HALVES
A_ALL = A_UNITS + 1
B_UNITS = GH * STEPS
RING = 3
Q_SLOTS = (0, 0, 0, 1, 1, 2)
K_SLOTS = (0, 1, 2, 0, 1, 0)
KROWS = HD * len(Q_SLOTS)
MROWS = 3
EPS = 1e-5
SCALE = float(HD) ** 0.5
RSQRT_MAGIC = 0x5F3759DF
N_CTRL = int(INTER * E / 128.9)
PIECES = INTER * E // (P * P)
A_AHEAD = (4, 5)
A_PER_STEP = [4, 4] + [5, 4, 4] * 3 + [4] * 2
assert sum(A_PER_STEP) == A_UNITS - sum(A_AHEAD) and len(A_PER_STEP) == STEPS - 3
DMA = 16
START = 1
PV_START = HALVES


def adaln_block(nc, x_in, w_qkv, b_qkv, w_proj, b_proj, gate_cp, up_cp, down_cp, c_in, w_mod, phase, ramp, out):
    att_dram = nc.dram_tensor("attention_scratch", [4, P, S], F32).ap()
    den_dram = nc.dram_tensor("denominator_scratch", [4, 2 * GH, S], F32).ap()

    keep = ExitStack()
    with keep:
        def sb(name, shape, dt=F32, where=keep):
            return where.enter_context(nc.sbuf_tensor(name, shape, dt))

        def sem(name):
            return keep.enter_context(nc.semaphore(name))

        ps = keep.enter_context(nc.psum_tensor("ps", [P, 8, BLK], F32))

        ident = sb("ident", [P, P])
        ident_bf = sb("ident_bf", [P, P], BF16)
        affine = sb("affine", [P, 4, EK, B])
        gates_raw = sb("gates_raw", [P, B, 2 * E])
        gates = sb("gates", [P, B, 2, E])
        windows = sb("windows", [P, 3, PIECES, 5])
        phase_sb = sb("phase_sb", [P, PIECES])
        ramp_sb = sb("ramp_sb", [P, P])
        spline_w = sb("spline_w", [P, 3, PIECES, P])

        a_mem = sb("a_mem", [P, 2 * TILES * E])
        with ExitStack() as until_last_group:
            q_parts = sb("q_parts", [P, 3, 2 * B * S], BF16, until_last_group)
            k_parts = sb("k_parts", [P, 3, 2 * B * S], BF16, until_last_group)
            v_all = sb("v_all", [P, 2, TILES, P], F32, until_last_group)
        gu_hi = sb("gu_hi", [P, 2, EK, INTER], F32R)
        gu_lo = sb("gu_lo", [P, 2, EK, INTER], F32R)
        dn_hi = sb("dn_hi", [P, IK, E], F32R)
        dn_lo = sb("dn_lo", [P, IK, E], F32R)
        wp_hi = sb("wp_hi", [P, EK, E], F32R)
        wp_lo = sb("wp_lo", [P, EK, E], F32R)
        att_hi = sb("att_hi", [P, EK, BLK], F32R)
        att_lo = sb("att_lo", [P, EK, BLK], F32R)
        res = sb("res", [P, TPB, E])
        with ExitStack() as until_last_group:
            qb0 = sb("qb0", [KROWS + MROWS, GH, S], BF16, until_last_group)
            kb0 = sb("kb0", [KROWS + MROWS, GH, S], BF16, until_last_group)
        h_full = sb("h_full2", [P, EK, BLK])
        h_hi = sb("h_hi2", [P, EK, BLK], F32R)
        h_lo = sb("h_lo2", [P, EK, BLK], F32R)
        sb("h_rest", [P, EK, BLK])
        x_in_a, xn_in_a = (a_mem[:, h * TILES * E:(h + 1) * TILES * E].rearrange("p (t e) -> p t e", t=TILES)
                           for h in range(2))

        qa, ka = ([a_mem[0:KROWS, (2 * n + p) * GH * S // 2:(2 * n + p + 1) * GH * S // 2].bitcast(BF16)
                   .rearrange("r (j s) -> r j s", j=GH) for p in range(2)] for n in range(2))
        a_loaded = [sem(f"a_loaded{p}") for p in range(2)]

        wm = spline_w[:, :, :, :].rearrange("p n m s -> p (n m s)")[:, 0:EK * 6 * E].rearrange("p (k f) -> p k f", k=EK)
        gates_flat = gates[:, :, :, :].rearrange("p b g e -> p (b g e)")
        silu_rep = gates_flat[:, 0:EK * B * P].rearrange("p (k b s) -> p k b s", k=EK, b=B)
        silu_c = gates_flat[:, EK * B * P:EK * B * (P + 1)].rearrange("p (k b) -> p k b", k=EK)
        wm_loaded = [sem(f"wm_loaded{n}") for n in range(2)]

        project_qkv(nc, locals())
        attention_and_mlp(nc, locals())


def names(scope, *wanted):
    return [scope[n] for n in wanted]


MODULATION = 2 * EK * EK


def modulate(nc, ps, bank, wm, silu_c, columns, n):
    v, k, kk = n // (EK * EK), n // EK % EK, n % EK
    at = (v * EK + k) * B
    return nc.tensor.matmul(ps[:, bank, at:at + B], wm[:, kk, columns[v] * E + k * P:columns[v] * E + (k + 1) * P],
                            silu_c[:, kk, :], start=(kk == 0), stop=(kk == EK - 1))


def mod_psum(ps, bank):
    return ps[:, bank, 0:2 * EK * B].rearrange("p (v k b) -> p v k b", v=2, k=EK)


def load_operands(sp, q_to, k_to, q_parts, k_parts, at, p, loaded):
    for to, parts, slots in ((q_to, q_parts, Q_SLOTS), (k_to, k_parts, K_SLOTS)):
        for r, part in enumerate(slots):
            sp.dma_start(to[HD * r:HD * r + HD], parts[64 * p:64 * p + 64, part, bass.ds(at, S)]).then_inc(loaded, DMA)


def project_qkv(nc, scope):
    (sem, x_in, w_qkv, b_qkv, c_in, w_mod, gate_cp, up_cp, down_cp, phase, ramp, ps, ident, ident_bf, affine, gates,
     windows, phase_sb, ramp_sb, spline_w, q_parts, k_parts, v_all, x_sb, xn, qa, ka, a_loaded, wm, wm_loaded,
     silu_c, silu_rep) = names(
        scope, "sem", "x_in", "w_qkv", "b_qkv", "c_in", "w_mod", "gate_cp", "up_cp", "down_cp", "phase", "ramp", "ps",
        "ident", "ident_bf", "affine", "gates", "windows", "phase_sb", "ramp_sb", "spline_w", "q_parts", "k_parts",
        "v_all", "x_in_a", "xn_in_a", "qa", "ka", "a_loaded", "wm", "wm_loaded",
        "silu_c", "silu_rep")
    FT = 6
    with ExitStack() as mem:
        def sb(name, shape, dt=F32):
            return mem.enter_context(nc.sbuf_tensor(name, shape, dt))

        w_rows = sb("w_rows", [P, FT, E])
        wt_hi = sb("wt_hi", [P, EK, FT * P], F32R)
        wt_lo = sb("wt_lo", [P, EK, FT * P], F32R)
        c_t = sb("c_t", [P, EK, B])
        bias_qk = sb("bias_qk", [P, 2, 2])
        bias_v = sb("bias_v", [P, E])
        stats = sb("stats", [P, TILES, 6])
        mean_var = sb("mean_var", [P, TILES, 2])
        var_eps = sb("var_eps", [P, TILES])
        std = sb("std", [P, TILES])
        rstd0 = sb("rstd0", [P, TILES])
        newton = sb("newton", [P, TILES])
        rstd = sb("rstd", [P, TILES])
        h_full = sb("h_full", [P, 2, EK, BLK])
        h_hi = sb("h_hi", [P, 2, EK, BLK], F32R)
        h_lo = sb("h_lo", [P, 2, EK, BLK], F32R)
        qk_full = sb("qk_full", [P, 2, BLK])
        qk_rest = sb("qk_rest", [P, 2, BLK])

        x_loaded = [sem(f"x_loaded{i}") for i in range(BLOCKS)]
        w_loaded = sem("w_loaded")
        c_loaded = sem("c_loaded")
        bias_loaded = sem("bias_loaded")
        spline_loaded = sem("spline_loaded")
        ident_ready = sem("ident_ready")
        pool_chain = sem("pool_chain")
        silu_ready = sem("silu_ready")
        silu_rep_ready = sem("silu_rep_ready")
        wt_made = sem("wt_made")
        wt_hi_ready = sem("wt_hi_ready")
        wt_ready = sem("wt_ready")
        mod_made = sem("mod_made")
        affine_ready = sem("affine_ready")
        dve_chain = sem("dve_chain")
        var_ready = sem("var_ready")
        std_ready = sem("std_ready")
        xn_ready = sem("xn_ready")
        xt_made = sem("xt_made")
        h_full_ready = sem("h_full_ready")
        h_hi_ready = sem("h_hi_ready")
        h_lo_ready = sem("h_lo_ready")
        qk_made = sem("qk_made")
        qk_full_ready = sem("qk_full_ready")
        part_h_ready = sem("part_h_ready")
        part_m_ready = sem("part_m_ready")
        part_l_ready = sem("part_l_ready")
        v_made = sem("v_made")
        v_ready = sem("v_ready")

        rows = w_qkv.rearrange("(h c d) e -> h c d e", c=3, d=HD)
        bias_rows = b_qkv.rearrange("(h c d) -> h c d", c=3, d=HD)
        WT_BANK = 4
        wt_banks = [[(t, 0) for t in range(4)], [(t, 1) for t in range(4)], [(4, 0), (5, 0), (4, 1), (5, 1)]]

        def tiles_of(i):
            return slice(TPB * i, TPB * i + TPB)

        def wt_view(w, n):
            if n < 2:
                return w[:, n, 0:4 * P]
            return w[:, :, 4 * P:6 * P]

        def wt_psum(n):
            bank = ps[:, WT_BANK + n, :]
            return bank if n < 2 else bank.rearrange("p (k f) -> p k f", k=EK)

        def load_tokens(queue, i):
            queue.dma_start(x_sb[:, TPB * i:TPB * i + TPB],
                            x_in[i * BLK:(i + 1) * BLK].rearrange("(t p) e -> p t e", p=P)).then_inc(x_loaded[i], DMA)

        def load_modulation(queue, n):
            columns = slice(2 * E * n, 6 * E if n else 2 * E)
            queue.dma_start(wm[:, :, columns], w_mod[:, columns].rearrange("(k p) f -> p k f", p=P))\
                 .then_inc(wm_loaded[n], DMA)

        with nc.Block() as block:

            @block.sync
            def _(sp):
                for comp in range(2):
                    for c in range(2):
                        for p in range(2):
                            src = rows[8 * c + 4 * p:8 * c + 4 * p + 4, comp].rearrange("j d e -> d j e")
                            sp.dma_start(w_rows[64 * p:64 * p + 64, 2 * comp + c, :], src).then_inc(w_loaded, DMA)
                for c in range(2):
                    sp.dma_start(w_rows[:, 4 + c, :], rows[8 * c:8 * c + 8, 2]).then_inc(w_loaded, DMA)
                load_tokens(sp, 1)
                with nc.allow_non_contiguous_dma(reason="biases by partition, once"):
                    for comp in range(2):
                        for c in range(2):
                            for p in range(2):
                                src = bias_rows[8 * c + 4 * p:8 * c + 4 * p + 4, comp].rearrange("j d -> d j")
                                sp.dma_start(bias_qk[64 * p:64 * p + 64, comp, c:c + 1], src).then_inc(bias_loaded, DMA)
                sp.dma_start(bias_v[:, :].rearrange("p (h d) -> p h d", d=HD),
                             bias_rows[:, 2, :].partition_broadcast(P)).then_inc(bias_loaded, DMA)
                for i in range(2, BLOCKS):
                    load_tokens(sp, i)
                load_modulation(sp, 1)
                for n, cp in enumerate((gate_cp, up_cp, down_cp)):
                    def piece(parts):
                        return bass.AP(cp.tensor, 0, [[1, parts], [P - 1, PIECES], [1, 5]])
                    sp.dma_start(windows[1:P, n], piece(P - 1)).then_inc(spline_loaded, DMA)
                    sp.dma_start(windows[0:1, n], piece(1)).then_inc(spline_loaded, DMA)
                sp.dma_start(phase_sb[:, :], phase).then_inc(spline_loaded, DMA)
                sp.dma_start(ramp_sb[:, :], ramp.partition_broadcast(P)).then_inc(spline_loaded, DMA)
                sp.wait_ge(part_l_ready, 4 * HALVES - 1)
                load_operands(sp, qa[0], ka[0], q_parts, k_parts, 0, 0, a_loaded[0])
                sp.wait_ge(bias_loaded, 9 * DMA)
                sp.wait_ge(spline_loaded, 8 * DMA)

            @block.gpsimd
            def _(pool):
                nc.gpsimd.memset(ident[:, :], 0.0).then_inc(pool_chain, 1)
                pool.wait_ge(pool_chain, 1)
                nc.gpsimd.affine_select(out=ident[:, :], in_=ident[:, :], compare_op=ALU.not_equal, fill=1.0,
                                        base=0, pattern=[[-1, P]], channel_multiplier=1).then_inc(pool_chain, 1)
                pool.wait_ge(pool_chain, 2)
                nc.gpsimd.tensor_copy(ident_bf[:, :], ident[:, :]).then_inc(ident_ready, 1)

                def h_low(i):
                    for k in range(EK):
                        pool.wait_ge(h_hi_ready, EK * i + k + 1)
                        if i >= 2:
                            pool.wait_ge(v_made, 2 * (i - 1))
                        nc.gpsimd.tensor_tensor(h_lo[:, i % 2, k], h_full[:, i % 2, k], h_hi[:, i % 2, k].bitcast(F32),
                                                ALU.subtract).then_inc(h_lo_ready, 1)

                h_low(0)
                for i in range(BLOCKS):
                    if i + 1 < BLOCKS:
                        h_low(i + 1)
                    for f in range(4):
                        n = 4 * i + f
                        parts = q_parts if f < 2 else k_parts
                        at = (f % 2) * B * S + i * BLK
                        pool.wait_ge(part_m_ready, n + 1)
                        nc.gpsimd.tensor_tensor(parts[:, 2, at:at + BLK], qk_rest[:, n % 2], parts[:, 1, at:at + BLK],
                                                ALU.subtract).then_inc(part_l_ready, 1)

            @block.scalar
            def _(act):
                with nc.allow_non_contiguous_dma(reason="the condition by partition, once"):
                    for b in range(B):
                        act.dma_start(c_t[:, :, b:b + 1].rearrange("p k b -> p (k b)"),
                                      c_in[b].rearrange("(k p) -> p k", p=P)).then_inc(c_loaded, DMA)
                load_tokens(act, 0)
                load_modulation(act, 0)
                act.wait_ge(c_loaded, B * DMA)
                nc.scalar.activation(silu_c[:, :, :], c_t[:, :, :], ACT.Silu).then_inc(silu_ready, 1)

                def root(i):
                    act.wait_ge(var_ready, i + 1)
                    nc.scalar.activation(std[:, tiles_of(i)], var_eps[:, tiles_of(i)], ACT.Sqrt).then_inc(std_ready, 1)

                root(0)
                root(1)
                for n in range(3):
                    act.wait_ge(wt_made, n + 1)
                    nc.scalar.copy(wt_view(wt_hi, n), wt_psum(n)).then_inc(wt_hi_ready, 1)

                def h_affine(i):
                    if i == 0:
                        act.wait_ge(affine_ready, 1)
                    b = i // 2
                    for k in range(EK):
                        act.wait_ge(xt_made, EK * i + k + 1)
                        if i >= 2:
                            act.wait_ge(h_lo_ready, EK * (i - 1))
                        nc.scalar.activation(h_full[:, i % 2, k], ps[:, k, :], ACT.Identity, bias=affine[:, 0, k, b:b + 1],
                                             scale=affine[:, 1, k, b:b + 1]).then_inc(h_full_ready, 1)

                h_affine(0)
                root(2)
                for i in range(BLOCKS):
                    if i + 1 < BLOCKS:
                        h_affine(i + 1)
                    for f in range(4):
                        if f == 2 and i + 3 < BLOCKS:
                            root(i + 3)
                        n = 4 * i + f
                        parts = q_parts if f < 2 else k_parts
                        at = (f % 2) * B * S + i * BLK
                        if n == 0:
                            act.wait_ge(bias_loaded, 9 * DMA)
                        act.wait_ge(qk_made, n + 1)
                        if n >= 2:
                            act.wait_ge(part_m_ready, n - 1)
                        nc.scalar.activation(qk_full[:, n % 2], ps[:, 2 + f, :], ACT.Identity,
                                             bias=bias_qk[:, f // 2, f % 2:f % 2 + 1]).then_inc(qk_full_ready, 1)
                        act.wait_ge(qk_full_ready, n + 1)
                        nc.scalar.copy(parts[:, 0, at:at + BLK], qk_full[:, n % 2]).then_inc(part_h_ready, 1)

            @block.vector
            def _(dve):
                done = [0]

                def link(ins):
                    done[0] += 1
                    ins.then_inc(dve_chain, 1)
                    dve.wait_ge(dve_chain, done[0])

                def layer_norm(i):
                    tiles = tiles_of(i)
                    dve.wait_ge(x_loaded[i], DMA)
                    for t in range(tiles.start, tiles.stop):
                        last = nc.vector.bn_stats(stats[:, t], x_sb[:, t])
                    link(last)
                    for t in range(tiles.start, tiles.stop):
                        last = nc.vector.bn_aggr(mean_var[:, t], stats[:, t])
                    link(last)
                    nc.vector.tensor_scalar(var_eps[:, tiles], mean_var[:, tiles, 1], EPS, None, ALU.add)\
                      .then_inc(var_ready, 1)
                    dve.wait_ge(std_ready, i + 1)
                    link(nc.vector.reciprocal(rstd0[:, tiles], std[:, tiles]))
                    link(nc.vector.tensor_tensor(newton[:, tiles], rstd0[:, tiles], rstd0[:, tiles], ALU.mult))
                    link(nc.vector.tensor_tensor(newton[:, tiles], newton[:, tiles], var_eps[:, tiles], ALU.mult))
                    link(nc.vector.tensor_scalar(newton[:, tiles], newton[:, tiles], -0.5, 1.5, ALU.mult, ALU.add))
                    link(nc.vector.tensor_tensor(rstd[:, tiles], rstd0[:, tiles], newton[:, tiles], ALU.mult))
                    for t in range(tiles.start, tiles.stop):
                        last = nc.vector.tensor_scalar(xn[:, t], x_sb[:, t], mean_var[:, t, 0:1], rstd[:, t:t + 1],
                                                       ALU.subtract, ALU.mult)
                    last.then_inc(xn_ready, 1)

                def h_high(i):
                    for k in range(EK):
                        dve.wait_ge(h_full_ready, EK * i + k + 1)
                        if i >= 2:
                            dve.wait_ge(v_made, 2 * (i - 1))
                        nc.vector.tensor_copy(h_hi[:, i % 2, k], h_full[:, i % 2, k]).then_inc(h_hi_ready, 1)

                dve.wait_ge(silu_ready, 1)
                nc.vector.tensor_copy(silu_rep[:, :, :, :],
                                      silu_c[:, :, :].unsqueeze(3).to_broadcast((P, EK, B, P))).then_inc(silu_rep_ready, 1)
                for i in range(2):
                    layer_norm(i)
                dve.wait_ge(mod_made, 1)
                link(nc.vector.tensor_copy(affine[:, 0:2], mod_psum(ps, 3)))
                nc.vector.tensor_scalar(affine[:, 1], affine[:, 1], 1.0, None, ALU.add).then_inc(affine_ready, 1)
                for n in range(3):
                    dve.wait_ge(wt_hi_ready, n + 1)
                    nc.vector.tensor_tensor(wt_view(wt_lo, n), wt_psum(n), wt_view(wt_hi, n).bitcast(F32),
                                            ALU.subtract).then_inc(wt_ready, 1)
                h_high(0)
                layer_norm(2)
                for i in range(BLOCKS):
                    if i + 1 < BLOCKS:
                        h_high(i + 1)
                    for f in range(4):
                        if f == 2 and i + 3 < BLOCKS:
                            layer_norm(i + 3)
                        n = 4 * i + f
                        parts = q_parts if f < 2 else k_parts
                        at = (f % 2) * B * S + i * BLK
                        dve.wait_ge(part_h_ready, n + 1)
                        if n >= 2:
                            dve.wait_ge(part_l_ready, n - 1)
                        link(nc.vector.tensor_tensor(qk_rest[:, n % 2], qk_full[:, n % 2], parts[:, 0, at:at + BLK],
                                                     ALU.subtract))
                        nc.vector.tensor_copy(parts[:, 1, at:at + BLK], qk_rest[:, n % 2]).then_inc(part_m_ready, 1)
                    for half in range(2):
                        n = 2 * i + half
                        dve.wait_ge(v_made, n + 1)
                        if n == 0:
                            dve.wait_ge(bias_loaded, 9 * DMA)
                        t = TPB * i + 2 * half
                        nc.vector.tensor_tensor(
                            v_all[:, :, t:t + 2, :].rearrange("p c t f -> p t c f"),
                            ps[:, 6 + half, :].rearrange("p (t c f) -> p t c f", t=2, c=2),
                            bias_v[:, :].rearrange("p (c f) -> p c f", c=2).unsqueeze(1).to_broadcast((P, 2, 2, P)),
                            ALU.add).then_inc(v_ready, 1)

            @block.tensor
            def _(pe):
                pe.wait_ge(ident_ready, 1)
                pe.wait_ge(w_loaded, 10 * DMA)
                for n, pairs in enumerate(wt_banks):
                    for m, (t, k) in enumerate(pairs):
                        last = nc.tensor.transpose(ps[:, WT_BANK + n, m * P:(m + 1) * P],
                                                   w_rows[:, t, k * P:(k + 1) * P], ident[:, :])
                    last.then_inc(wt_made, 1)
                pe.wait_ge(silu_ready, 1)
                pe.wait_ge(wm_loaded[0], DMA)
                for n in range(MODULATION):
                    last = modulate(nc, ps, 3, wm, silu_c, (0, 1), n)
                last.then_inc(mod_made, 1)

                def transpose_block(i):
                    pe.wait_ge(xn_ready, i + 1)
                    if i:
                        pe.wait_ge(h_full_ready, EK * i)
                    for k in range(EK):
                        for t in range(TPB):
                            last = nc.tensor.transpose(ps[:, k, t * P:(t + 1) * P], xn[:, TPB * i + t, k * P:(k + 1) * P],
                                                       ident[:, :])
                        last.then_inc(xt_made, 1)

                transpose_block(0)
                pe.wait_ge(affine_ready, 1)
                pe.wait_ge(wt_ready, 3)
                for i in range(BLOCKS):
                    if i + 1 < BLOCKS:
                        transpose_block(i + 1)
                    pe.wait_ge(h_lo_ready, EK * (i + 1))
                    for f in range(4):
                        if i:
                            pe.wait_ge(qk_full_ready, 4 * (i - 1) + f + 1)
                        for k in range(EK):
                            for a, (w, h) in enumerate(((wt_hi, h_hi), (wt_hi, h_lo), (wt_lo, h_hi))):
                                last = nc.tensor.matmul(ps[:, 2 + f, :], w[:, k, f * P:(f + 1) * P], h[:, i % 2, k],
                                                        start=(k == 0 and a == 0), stop=(k == EK - 1 and a == 2))
                        last.then_inc(qk_made, 1)
                    for half in range(2):
                        if i:
                            pe.wait_ge(v_ready, 2 * (i - 1) + half + 1)
                        for t in range(2):
                            tok = slice((2 * half + t) * P, (2 * half + t + 1) * P)
                            for k in range(EK):
                                for a, (h, w) in enumerate(((h_hi, wt_hi), (h_hi, wt_lo), (h_lo, wt_hi))):
                                    last = nc.tensor.matmul(ps[:, 6 + half, t * E:(t + 1) * E], h[:, i % 2, k, tok],
                                                            w[:, k, 4 * P:6 * P],
                                                            start=(k == 0 and a == 0), stop=(k == EK - 1 and a == 2))
                        last.then_inc(v_made, 1)


def attention_and_mlp(nc, scope):
    (sem, x_in, w_proj, b_proj, out, qb0, kb0, h_full, h_hi, h_lo, wm, wm_loaded, silu_c, silu_rep,
     qa, ka, a_loaded, gates_raw, ps, ident, ident_bf, affine, gates, q_parts, k_parts, v_all, windows, phase_sb,
     ramp_sb, spline_w, a_mem, gu_hi, gu_lo, dn_hi, dn_lo, wp_hi, wp_lo, att_hi, att_lo, res, att_dram, den_dram) = names(
        scope, "sem", "x_in", "w_proj", "b_proj", "out", "qb0", "kb0", "h_full", "h_hi", "h_lo", "wm", "wm_loaded",
        "silu_c", "silu_rep", "qa", "ka", "a_loaded", "gates_raw", "ps", "ident", "ident_bf", "affine", "gates", "q_parts",
        "k_parts", "v_all", "windows", "phase_sb", "ramp_sb", "spline_w", "a_mem", "gu_hi",
        "gu_lo", "dn_hi", "dn_lo", "wp_hi", "wp_lo", "att_hi", "att_lo", "res", "att_dram", "den_dram")
    with ExitStack() as kept:
        def sb_kept(name, shape, dt=F32):
            return kept.enter_context(nc.sbuf_tensor(name, shape, dt))

        heads = [sb_kept(f"heads{p}", [P, HALVES, BLK]) for p in range(2)]
        wp = sb_kept("wp", [P, EK, E])
        bp = sb_kept("bp", [P, E])
        DEN_COLS = 2 * GH * S // P
        den = sb_kept("den", [P, B, EK, DEN_COLS])
        stats = sb_kept("stats2", [P, TPB, 6])
        mean_var = sb_kept("mean_var2", [P, TPB, 2])
        var_eps = sb_kept("var_eps2", [P, TPB])
        guess = sb_kept("guess", [P, TPB], I32)
        newton = sb_kept("newton2", [P, TPB])
        rstd = sb_kept("rstd2", [P, TPB])

        def take(start, a, b):
            return a_mem[:, start:start + a * b].rearrange("p (a b) -> p a b", a=a)

        SLAB = EK * BLK
        x_sb = take(0, TILES, E)
        att = take(TILES * E, EK, BLK)
        inverse = take(TILES * E + SLAB, EK, BLK)
        att_norm = take(TILES * E + 2 * SLAB, EK, BLK)
        xn = take(TILES * E + 3 * SLAB, TPB, E)

        heads_ready = sem("heads_ready")
        heads_stored = [sem(f"heads_stored{p}") for p in range(2)]
        wp_loaded = sem("wp_loaded")
        bp_loaded = sem("bp_loaded")
        x2_loaded = sem("x2_loaded")
        den_loaded = sem("den_loaded")
        den_inverted = sem("den_inverted")
        inverses_stored = sem("inverses_stored")
        att_loaded = sem("att_loaded")
        tr_made = sem("tr_made")
        tr_hi = sem("tr_hi")
        tr_lo = sem("tr_lo")
        att_hi_ready = sem("att_hi_ready")
        att_ready = sem("att_ready")
        proj_made = sem("proj_made")
        proj_read = sem("proj_read")
        chain = sem("mlp_chain")
        xn_ready = sem("xn_ready2")
        xt_made = sem("xt_made2")
        h_full_ready = sem("h_full_ready2")
        h_hi_ready = sem("h_hi_ready2")
        h_ready = sem("h_ready2")
        gu_made = sem("gu_made")
        silu_ready = sem("silu_ready2")
        inter_ready = sem("inter_ready")
        in_hi_ready = sem("in_hi_ready")
        in_ready = sem("in_ready")
        down_made = sem("down_made")
        down_read = sem("down_read")
        y_ready = sem("y_ready")
        y_stored = sem("y_stored")

        G_BANK, D_BANK, X_BANK = 0, 4, 6
        PROJECT_AT = 1
        TR = 3 * PIECES // 4 + 1
        T_RING = 3
        HEADS_STEP, PROJECT_STEP = 3, 7
        LAST_GROUP = {}
        LAST_RING = []
        for n in range(1, TR + 2):
            if n == PROJECT_STEP:
                LAST_RING += [("projection", half) for half in range(2)]
            else:
                LAST_GROUP[n] = len(LAST_GROUP)
                LAST_RING.append(("weights", LAST_GROUP[n]))
        LAST_RING += [("tokens", k) for k in range(EK)]

        def ring_bank(kind, n):
            return LAST_RING.index((kind, n)) % T_RING

        PROJECT_AFTER = LAST_GROUP[PROJECT_STEP - 1]
        PROJECT_BANKS = [ring_bank("projection", half) for half in range(2)]
        TOKEN_BANKS = [ring_bank("tokens", k) for k in range(EK)]

        def prod(a, b):
            return (a[0], b[0]), (a[0], b[1]), (a[1], b[0])

        def tr_out(n, w):
            if n == 0:
                return w[2][:, :, :].rearrange("p k (r e) -> p r k e", r=2)
            n -= 1
            weight, m = n // 4, 4 * (n % 4)
            if weight < 2:
                return w[0][:, weight, :, m * 64:(m + 4) * 64].rearrange("p k i -> p i k")
            return w[1][:, :, m * 16:(m + 4) * 16].rearrange("p i o -> p o i")

        def tr_in(n):
            bank = ps[:, ring_bank("weights", n), :]
            if n == 0:
                return bank.rearrange("p (r k e) -> p r k e", r=2, k=EK)
            if (n - 1) // 4 < 2:
                return bank.rearrange("p (i k) -> p i k", k=EK)
            return bank.rearrange("p (o i) -> p o i", i=IK)

        def store_heads(it, p):
            for j in range(GH):
                at = 64 * p + HD * j
                nc.sync.dma_start(att_dram[bass.ds(it, 1), at:at + HD, :], heads[p][32 * j:32 * j + HD])\
                  .then_inc(heads_stored[p], DMA)
                nc.sync.dma_start(den_dram[bass.ds(it, 1), GH * p + j:GH * p + j + 1, :],
                             heads[p][32 * j + HD:32 * j + HD + 1]).then_inc(heads_stored[p], DMA)

        def den_rows(b, c):
            return den_dram[b + 2 * c].rearrange("g (q s) -> (g q) s", s=DEN_COLS)

        def load_denominators(b):
            for c in range(EK):
                nc.sync.dma_start(den[:, b, c, :], den_rows(b, c)).then_inc(den_loaded, DMA)

        def invert_denominators(b):
            nc.vector.wait_ge(den_loaded, (b + 1) * EK * DMA)
            nc.vector.reciprocal(den[:, b], den[:, b]).then_inc(den_inverted, 1)

        def store_inverses(b):
            nc.sync.wait_ge(den_inverted, b + 1)
            for c in range(EK):
                nc.sync.dma_start(den_rows(b, c), den[:, b, c, :]).then_inc(inverses_stored, DMA)
            nc.sync.wait_ge(inverses_stored, (b + 1) * EK * DMA)

        def load_att(i, b, half):
            for c in range(EK):
                part = b + 2 * c
                tokens = slice(half * BLK, (half + 1) * BLK)
                nc.sync.dma_start(inverse[:, c, :], den_dram[part, :, tokens].unsqueeze(1).to_broadcast((2 * GH, HD, BLK)))\
                  .then_inc(att_loaded, DMA)
                nc.sync.dma_start(att[:, c, :], att_dram[part, :, tokens]).then_inc(att_loaded, DMA)

        def project_tile(i, t, bank):
            if t == 0:
                nc.tensor.wait_ge(att_ready, (i + 1) * EK)
            for k in range(EK):
                for a, (x, w) in enumerate(prod((att_hi, att_lo), (wp_hi, wp_lo))):
                    last = nc.tensor.matmul(ps[:, bank, (t % 2) * E:(t % 2 + 1) * E], x[:, k, t * P:(t + 1) * P], w[:, k, :],
                                            start=(k == 0 and a == 0), stop=(k == EK - 1 and a == 2))
            if t % 2:
                last.then_inc(proj_made, 1)

        def transpose_tokens(i, k, bank):
            for t in range(TPB):
                last = nc.tensor.transpose(ps[:, bank, t * P:(t + 1) * P], xn[:, t, k * P:(k + 1) * P], ident[:, :])
            last.then_inc(xt_made, 1)

        done = [0]

        def link(ins):
            done[0] += 1
            ins.then_inc(chain, 1)
            nc.vector.wait_ge(chain, done[0])

        def att_high(i, c):
            nc.vector.wait_ge(att_loaded, (i + 1) * (EK * 2 * DMA))
            if i:
                nc.vector.wait_ge(att_ready, EK * i)
            link(nc.vector.tensor_tensor(att_norm[:, c], att[:, c], inverse[:, c], ALU.mult))
            if i:
                nc.vector.wait_ge(proj_made, 2 * i)
            nc.vector.tensor_copy(att_hi[:, c], att_norm[:, c]).then_inc(att_hi_ready, 1)

        def project_gated(i, b, half, banks=(X_BANK, X_BANK + 1)):
            nc.vector.wait_ge(proj_made, 2 * i + half + 1)
            part = res[:, 2 * half:2 * half + 2, :]
            nc.vector.tensor_tensor(part, ps[:, banks[half], :].rearrange("p (t e) -> p t e", t=2),
                                    bp[:, :].unsqueeze(1).to_broadcast((P, 2, E)), ALU.add).then_inc(proj_read, 1)
            nc.vector.wait_ge(proj_read, 2 * i + half + 1)
            link(nc.vector.tensor_tensor(part, part, gates[:, b, 0, :].unsqueeze(1).to_broadcast((P, 2, E)),
                                         ALU.mult))

        def residual(i, half):
            x = x_sb[:, TPB * i + 2 * half:TPB * i + 2 * half + 2, :]
            link(nc.vector.tensor_tensor(x, x, res[:, 2 * half:2 * half + 2, :], ALU.add))
            for t in range(2 * half, 2 * half + 2):
                last = nc.vector.bn_stats(stats[:, t], x_sb[:, TPB * i + t])
            link(last)

        def inverse_deviation():
            for t in range(TPB):
                last = nc.vector.bn_aggr(mean_var[:, t], stats[:, t])
            link(last)
            link(nc.vector.tensor_scalar(var_eps[:, :], mean_var[:, :, 1], EPS, None, ALU.add))
            link(nc.vector.tensor_scalar(guess[:, :], var_eps[:, :].bitcast(I32), 1, None, ALU.logical_shift_right))
            link(nc.vector.tensor_scalar(guess[:, :], guess[:, :], -1.0, float(RSQRT_MAGIC), ALU.mult, ALU.add))
            link(nc.vector.tensor_scalar(var_eps[:, :], var_eps[:, :], -0.5, None, ALU.mult))
            root = guess[:, :].bitcast(F32)
            for _ in range(3):
                link(nc.vector.tensor_tensor(newton[:, :], root, root, ALU.mult))
                link(nc.vector.tensor_tensor(newton[:, :], newton[:, :], var_eps[:, :], ALU.mult))
                link(nc.vector.scalar_tensor_tensor(out=rstd[:, :], in0=newton[:, :], scalar=1.5, in1=root, op0=ALU.add,
                                                    op1=ALU.mult))
                root = rstd[:, :]

        def normalise(i):
            for t in range(TPB):
                last = nc.vector.tensor_scalar(xn[:, t], x_sb[:, TPB * i + t], mean_var[:, t, 0:1], rstd[:, t:t + 1],
                                               ALU.subtract, ALU.mult)
            last.then_inc(xn_ready, 1)

        def h_parts(i):
            for k in range(EK):
                nc.vector.wait_ge(h_full_ready, i * EK + k + 1)
                nc.vector.tensor_copy(h_hi[:, k], h_full[:, k]).then_inc(h_hi_ready, 1)
                nc.vector.wait_ge(h_hi_ready, i * EK + k + 1)
                nc.vector.tensor_tensor(h_lo[:, k], h_full[:, k], h_hi[:, k].bitcast(F32), ALU.subtract)\
                  .then_inc(h_ready, 1)

        def h_affine(i, b, banks=(X_BANK, X_BANK + 1)):
            for k in range(EK):
                nc.scalar.wait_ge(xt_made, i * EK + (k + 1))
                nc.scalar.activation(h_full[:, k], ps[:, banks[k], :], ACT.Identity, bias=affine[:, 2, k, b:b + 1],
                                     scale=affine[:, 3, k, b:b + 1]).then_inc(h_full_ready, 1)

        def att_low(i, chunks=range(EK)):
            for c in chunks:
                nc.gpsimd.wait_ge(att_hi_ready, EK * i + c + 1)
                nc.gpsimd.tensor_tensor(att_lo[:, c], att_norm[:, c], att_hi[:, c].bitcast(F32), ALU.subtract)\
                  .then_inc(att_ready, 1)

        with ExitStack() as mem:
            def sb(name, shape, dt=F32):
                return mem.enter_context(nc.sbuf_tensor(name, shape, dt))

            qb = [qb0, sb("qb1", [KROWS + MROWS, GH, S], BF16)]
            kb = [kb0, sb("kb1", [KROWS + MROWS, GH, S], BF16)]
            vg = [sb(f"vg{p}", [P, KT, GH, 2 * HD]) for p in range(2)]
            probs = sb("probs", [P, 2, GH, BLK])
            max_parts = sb("max_parts", [P, GH * KT, HALVES])
            neg_max = sb("neg_max", [P, GH * KT])
            rest = sb("rest", [P, 2, GH * KT])
            neg_split = sb("neg_split", [P, MROWS, GH * KT], BF16)
            neg_rows = sb("neg_rows", [MROWS * GH * KT, P], BF16)
            coef = sb("coef", [P, 6, 3, PIECES])
            diff = sb("diff", [P, 3, PIECES, 10])
            z = sb("z", [P, 4, P])
            y = sb("y", [P, 4, P])
            bend = gates_raw[:, 0, :].rearrange("p (m s) -> p m s", m=4)

            b_loaded = [sem(f"b_loaded{p}") for p in range(2)]
            v_loaded = [sem(f"v_loaded{p}") for p in range(2)]
            max_loaded = [sem(f"max_loaded{p}") for p in range(2)]
            ones_ready = sem("ones_ready")
            a_full = sem("a_full")
            a_free = sem("a_free")
            neg_ready = sem("neg_ready")
            max_chain = sem("max_chain")
            b_full = sem("b_full")
            p_ready = sem("p_ready")
            pv_done = sem("pv_done")
            spline_chain = sem("spline_chain")
            spline_ready = sem("spline_ready")
            gates_made = sem("gates_made")
            mod_made2 = sem("mod_made2")
            vectors_raw = sem("vectors_raw")
            guard_ready = sem("guard_ready")

            SLOTS = len(Q_SLOTS)
            A_BANK, B_BANK, O_BANK = 0, RING, 2 * RING

            def b_bank(p, u):
                return B_BANK + (u + p) % RING

            COPY_AT = (2, 5)
            MOD_BANK = O_BANK
            GATES = B * 2 * EK
            v_view = v_all[:, :, :, :].rearrange("p c (b k) (g j d) -> p (c b) k g (j d)", b=B, g=2, j=GH)
            neg_psum = ps[:, A_BANK + A_UNITS % RING, :].bitcast(BF16)[0:MROWS * GH * KT, 0:P]

            with nc.Block() as block:

                @block.sync
                def _(sp):
                    def load_b(it, at, p):
                        load_operands(sp, qb[p], kb[p], q_parts, k_parts, at, p, b_loaded[p])
                        for kt in range(KT):
                            sp.dma_start(vg[p][:, kt, :, 0:HD],
                                         v_view[:, bass.ds(it, 1), kt, p, :].rearrange("p o (j d) -> p (o j) d", j=GH))\
                              .then_inc(v_loaded[p], DMA)

                    def load_max(p):
                        sp.dma_start(qb[p][KROWS:KROWS + MROWS], neg_rows[:, :]).then_inc(max_loaded[p], DMA)

                    def in_register(value, most=1 << 16):
                        return sp.snap(sp.to_reg(value), min_val=0, max_val=most)

                    def pair(it, number, last):
                        this, this_at = number(it, 2), number(it * S, 2 * S)
                        after, after_at = (None, None) if last else (number(it + 1, 3), number((it + 1) * S, 3 * S))
                        a_issued = [number((it * 2 + p + 1) * A_ALL) for p in range(2)]
                        pv_issued = [number((it * 2 + p) * STEPS + PV_START) for p in range(2)]
                        a_read = [number((it * 2 + p + 2) * A_ALL) for p in range(2)]
                        heads_read = [number((it * 2 + p + 1) * HALVES + PV_START) for p in range(2)]
                        for p in range(2):
                            sp.wait_ge(a_full, a_issued[p])
                            if not last:
                                load_operands(sp, qa[p], ka[p], q_parts, k_parts, after_at, p, a_loaded[p])
                            if not last or p == 0:
                                sp.wait_ge(pv_done, pv_issued[p])
                                load_b(after if p else this, after_at if p else this_at, 1 - p)
                                if last:
                                    for parity in range(2):
                                        sp.wait_ge(heads_stored[parity], 3 * 2 * GH * DMA + DMA)
                                    load_denominators(0)
                                sp.wait_ge(a_free, a_read[p])
                                load_max(1 - p)
                                if last:
                                    store_inverses(0)
                                    load_att(0, 0, 0)
                            if last and p:
                                sp.dma_start(x_sb, x_in.rearrange("(t p) e -> p t e", p=P)).then_inc(x2_loaded, DMA)
                                sp.wait_ge(att_ready, EK)
                                load_att(1, 0, 1)
                            if not last or p == 0:
                                sp.wait_ge(heads_ready, heads_read[p])
                                store_heads(this, p)

                    for p in range(2):
                        sp.sem_inc(heads_stored[p], DMA)
                    load_b(0, 0, 0)
                    load_operands(sp, qa[1], ka[1], q_parts, k_parts, 0, 1, a_loaded[1])
                    sp.dma_start(wp[:, :, :], w_proj.rearrange("(r p) e -> p r e", p=P)).then_inc(wp_loaded, DMA)
                    sp.dma_start(bp[:, :], b_proj.partition_broadcast(P)).then_inc(bp_loaded, DMA)
                    sp.wait_ge(a_free, A_ALL)
                    load_max(0)
                    with sp.Fori(0, GROUPS // 2 - 1) as it:
                        pair(it, in_register, False)
                    pair(GROUPS // 2 - 1, lambda value, most=0: value, True)

                @block.tensor
                def _(pe):
                    def a_unit(it, p, u, bank=None):
                        g = it * 2 + p
                        j, t, half = u // (KT * HALVES), u // HALVES % KT, u % HALVES
                        if u == 0:
                            pe.wait_ge(a_loaded[p], (it + 1) * (2 * SLOTS * DMA))
                        if u < 2 and not (isinstance(g, int) and g == 0):
                            pe.wait_ge(a_free, g * A_ALL + (u - 1))
                        if bank is None and u >= RING:
                            pe.wait_ge(a_free, g * A_ALL + (u - RING + 1))
                        elif bank is not None and u >= 2 * RING and u % 2 == 0:
                            pe.wait_ge(a_free, u - 2 * RING + 2)
                        nc.tensor.matmul(ps[:, A_BANK + u % RING if bank is None else bank, :], qa[p][:, j, t * P:(t + 1) * P],
                                         ka[p][:, j, half * BLK:(half + 1) * BLK], start=True, stop=True).then_inc(a_full, 1)

                    def max_transpose(it, p):
                        pe.wait_ge(neg_ready, it * 2 + (p + 1))
                        nc.tensor.transpose(neg_psum, neg_split[:, :, :].rearrange("p m u -> p (m u)"), ident_bf[:, :])\
                          .then_inc(a_full, 1)

                    def b_unit(it, p, n, j):
                        g = it * 2 + p
                        u, kt, half = GH * n + j, n // HALVES, n % HALVES
                        if u == 0:
                            pe.wait_ge(b_loaded[p], (it + 1) * (2 * SLOTS * DMA))
                            pe.wait_ge(max_loaded[p], (it + 1) * DMA)
                        if u >= RING:
                            pe.wait_ge(p_ready, g * B_UNITS + (u - RING + 1))
                        elif not (isinstance(g, int) and g == 0):
                            before = max(v for v in range(B_UNITS) if b_bank(1 - p, v) == b_bank(p, u))
                            pe.wait_ge(p_ready, g * B_UNITS - (B_UNITS - 1 - before))
                        nc.tensor.matmul(ps[:, b_bank(p, u), :], kb[p][:, j, kt * P:(kt + 1) * P],
                                         qb[p][:, j, half * BLK:(half + 1) * BLK], start=True, stop=True).then_inc(b_full, 1)

                    def pv(it, p, n):
                        g = it * 2 + p
                        kt, half = n // HALVES, n % HALVES
                        if n == 0:
                            pe.wait_ge(v_loaded[p], (it + 1) * (KT * DMA))
                        if n < HALVES:
                            pe.wait_ge(heads_ready, g * HALVES + (half + 1))
                        pe.wait_ge(p_ready, g * B_UNITS + GH * (n + 1))
                        for j in range(GH):
                            last = nc.tensor.matmul(ps[32 * j:32 * j + 32, O_BANK + half, :], vg[p][:, kt, j, :],
                                                    probs[:, n % 2, j, :], start=(kt == 0), stop=(kt == KT - 1))
                        last.then_inc(pv_done, 1)

                    def wait_ring(kind, n):
                        before = LAST_RING.index((kind, n)) - T_RING
                        if before < 0:
                            pe.wait_ge(a_free, GROUPS * A_ALL)
                        elif LAST_RING[before][0] == "weights":
                            pe.wait_ge(tr_lo, LAST_RING[before][1] + 1)
                        elif LAST_RING[before][0] == "projection":
                            pe.wait_ge(proj_read, LAST_RING[before][1] + 1)
                        else:
                            pe.wait_ge(h_full_ready, LAST_RING[before][1] + 1)

                    def weight_transpose(n, m):
                        if m == 0:
                            wait_ring("weights", n)
                        if n == 0:
                            src = wp[:, m // 2, (m % 2) * P:(m % 2 + 1) * P]
                        else:
                            src = spline_w[:, (n - 1) // 4, 4 * ((n - 1) % 4) + m, :]
                        made = nc.tensor.transpose(ps[:, ring_bank("weights", n), m * P:(m + 1) * P], src, ident[:, :])
                        if m == 3:
                            made.then_inc(tr_made, 1)

                    def start_group(it, p, it_a, p_a):
                        u = A_AHEAD[0]
                        for j in range(GH):
                            b_unit(it, p, 0, j)
                            for _ in range(0 if it_a is None else A_AHEAD[1] * (j + 1) // GH - A_AHEAD[1] * j // GH):
                                a_unit(it_a, p_a, u)
                                u += 1

                    def group(it, p, after_next=True):
                        it_a, p_a = it + p, 1 - p
                        u = sum(A_AHEAD)
                        for n in range(1, STEPS):
                            for j in range(GH):
                                b_unit(it, p, n, j)
                                if n - 1 < len(A_PER_STEP):
                                    share = A_PER_STEP[n - 1]
                                    for _ in range(share * (j + 1) // GH - share * j // GH):
                                        a_unit(it_a, p_a, u)
                                        u += 1
                                elif n == STEPS - 1 and after_next:
                                    a_unit(it + 1, p, j)
                            pv(it, p, n - 1)
                            if n == STEPS - 2:
                                max_transpose(it_a, p_a)
                        start_group(it_a, p_a, it + 1 if after_next else None, p)
                        pv(it, p, STEPS - 1)

                    def last_group(it, p):
                        pe.wait_ge(wp_loaded, DMA)
                        pe.wait_ge(spline_ready, 1)
                        for n in range(1, STEPS):
                            for j in range(GH):
                                b_unit(it, p, n, j)
                                if n == PROJECT_STEP:
                                    if j == 0:
                                        pe.wait_ge(tr_lo, 1)
                                    if j % 2 == 0:
                                        wait_ring("projection", j // 2)
                                    project_tile(0, j, PROJECT_BANKS[j // 2])
                                elif n in LAST_GROUP:
                                    weight_transpose(LAST_GROUP[n], j)
                            pv(it, p, n - 1)
                        pv(it, p, STEPS - 1)
                        pe.wait_ge(xn_ready, 1)
                        for k in range(EK):
                            wait_ring("tokens", k)
                            transpose_tokens(0, k, TOKEN_BANKS[k])

                    pe.sem_inc(pv_done, PV_START)
                    pe.wait_ge(wm_loaded[1], DMA)
                    for u in range(A_UNITS):
                        a_unit(0, 0, u, A_BANK + u % (2 * RING))
                        n = u // 2
                        if u % 2 and n < GATES:
                            b, g, kk = n // (2 * EK), n // EK % 2, n % EK
                            column = (2, 5)[g]
                            made = nc.tensor.matmul(ps[:, O_BANK + b, g * E:(g + 1) * E], silu_rep[:, kk, b, :],
                                                    wm[:, kk, column * E:(column + 1) * E],
                                                    start=(kk == 0), stop=(kk == EK - 1))
                            if n == GATES - 1:
                                made.then_inc(gates_made, 1)
                        elif u % 2 and n < GATES + MODULATION:
                            if n == GATES:
                                pe.wait_ge(vectors_raw, B)
                            made = modulate(nc, ps, MOD_BANK, wm, silu_c, (3, 4), n - GATES)
                            if n == GATES + MODULATION - 1:
                                made.then_inc(mod_made2, 1)
                    max_transpose(0, 0)
                    for u in range(A_AHEAD[0]):
                        a_unit(0, 1, u)
                    pe.wait_ge(ones_ready, 4)
                    pe.wait_ge(guard_ready, 1)
                    start_group(0, 0, 0, 1)
                    with pe.Fori(0, GROUPS // 2 - 1) as it:
                        group(it, 0)
                        group(it, 1)
                    group(GROUPS // 2 - 1, 0, after_next=False)
                    last_group(GROUPS // 2 - 1, 1)

                @block.vector
                def _(dve):
                    CHAIN = 5

                    def maxima(g):
                        for u in range(A_UNITS):
                            dve.wait_ge(a_full, g * A_ALL + (u + 1))
                            nc.vector.tensor_reduce(max_parts[:, u // HALVES, u % HALVES:u % HALVES + 1],
                                                    ps[:, A_BANK + u % RING, :], AX, ALU.max).then_inc(a_free, 1)
                        dve.wait_ge(a_free, g * A_ALL + A_UNITS)
                        split_maxima(g, max_parts[:, :, :])

                    def first_maxima():
                        for t in range(GH * KT):
                            at = A_BANK + HALVES * (t % RING)
                            dve.wait_ge(a_full, HALVES * (t + 1))
                            nc.vector.tensor_reduce(max_parts[:, t, 0:1], ps[:, at:at + HALVES, :],
                                                    mybir.AxisListType.XY, ALU.max).then_inc(a_free, HALVES)
                        dve.wait_ge(a_free, A_UNITS)
                        split_maxima(0, max_parts[:, :, 0:1])

                    def split_maxima(g, parts):
                        done = [0]

                        def link(ins):
                            done[0] += 1
                            ins.then_inc(max_chain, 1)
                            dve.wait_ge(max_chain, g * CHAIN + done[0])

                        link(nc.vector.tensor_reduce(neg_max[:, :], parts, AX, ALU.max, negate=True))
                        link(nc.vector.tensor_copy(neg_split[:, 0], neg_max[:, :]))
                        link(nc.vector.tensor_tensor(rest[:, 0], neg_max[:, :], neg_split[:, 0], ALU.subtract))
                        link(nc.vector.tensor_copy(neg_split[:, 1], rest[:, 0]))
                        link(nc.vector.tensor_tensor(rest[:, 1], rest[:, 0], neg_split[:, 1], ALU.subtract))
                        assert done[0] == CHAIN
                        nc.vector.tensor_copy(neg_split[:, 2], rest[:, 1]).then_inc(neg_ready, 1)
                        dve.wait_ge(a_full, (g + 1) * A_ALL)
                        nc.vector.tensor_copy(neg_rows[:, :], neg_psum).then_inc(a_free, 1)

                    first_maxima()
                    with dve.Fori(0, GROUPS // 2 - 1) as it:
                        maxima(it * 2 + 1)
                        maxima(it * 2 + 2)
                    maxima(GROUPS - 1)
                    invert_denominators(0)
                    dve.sem_inc(down_read, START)
                    dve.wait_ge(b_loaded[1], GROUPS // 2 * 2 * SLOTS * DMA)
                    dve.wait_ge(v_loaded[1], GROUPS // 2 * KT * DMA)
                    for n in range(TR):
                        dve.wait_ge(tr_made, n + 1)
                        nc.vector.tensor_copy(tr_out(n, (gu_hi, dn_hi, wp_hi)), tr_in(n)).then_inc(tr_hi, 1)
                        dve.wait_ge(tr_hi, n + 1)
                        nc.vector.tensor_tensor(tr_out(n, (gu_lo, dn_lo, wp_lo)), tr_in(n),
                                                tr_out(n, (gu_hi, dn_hi, wp_hi)).bitcast(F32), ALU.subtract).then_inc(tr_lo, 1)
                        if HEADS_STEP <= n < HEADS_STEP + EK:
                            att_high(0, n - HEADS_STEP)
                        elif n == PROJECT_AFTER:
                            dve.wait_ge(bp_loaded, DMA)
                            for half in range(2):
                                project_gated(0, 0, half, PROJECT_BANKS)
                        elif n in (PROJECT_AFTER + 1, PROJECT_AFTER + 2):
                            dve.wait_ge(x2_loaded, DMA)
                            residual(0, n - PROJECT_AFTER - 1)
                        elif n == PROJECT_AFTER + 3:
                            inverse_deviation()
                    normalise(0)
                    for c in range(EK):
                        att_high(1, c)
                    h_parts(0)

                @block.scalar
                def _(act):
                    def copy_heads(it, p, half):
                        g = it * 2 + p
                        act.wait_ge(pv_done, g * STEPS + (STEPS - HALVES + half + 1 + PV_START))
                        if half == 0:
                            act.wait_ge(heads_stored[p], it * (2 * GH * DMA) + DMA)
                        nc.scalar.copy(heads[p][:, half, :], ps[:, O_BANK + half, :]).then_inc(heads_ready, 1)

                    def exponentials(it, p, before):
                        g = it * 2 + p
                        for u in range(B_UNITS):
                            n, j = u // GH, u % GH
                            if before and u in COPY_AT:
                                copy_heads(*before, COPY_AT.index(u))
                            act.wait_ge(b_full, g * B_UNITS + (u + 1))
                            if j == 0:
                                act.wait_ge(pv_done, g * STEPS + (n - 1 + PV_START))
                            nc.scalar.activation(probs[:, n % 2, j, :], ps[:, b_bank(p, u), :], ACT.Exp,
                                                 scale=SCALE).then_inc(p_ready, 1)

                    act.preload_act_table(ACT.Exp)
                    act.wait_ge(gates_made, 1)
                    for b in range(B):
                        nc.scalar.copy(gates_raw[:, b], ps[:, O_BANK + b, :]).then_inc(vectors_raw, 1)
                    act.wait_ge(mod_made2, 1)
                    nc.scalar.copy(affine[:, 2:4], mod_psum(ps, MOD_BANK)).then_inc(vectors_raw, 1)
                    act.sem_inc(heads_ready, PV_START)
                    exponentials(0, 0, None)
                    with act.Fori(0, GROUPS // 2 - 1) as it:
                        exponentials(it, 1, (it, 0))
                        exponentials(it + 1, 0, (it, 1))
                    exponentials(GROUPS // 2 - 1, 1, (GROUPS // 2 - 1, 0))
                    act.preload_act_table(ACT.Silu)
                    h_affine(0, 0, TOKEN_BANKS)
                    for half in range(HALVES):
                        copy_heads(GROUPS // 2 - 1, 1, half)

                @block.gpsimd
                def _(pool):
                    done = [0]

                    def link(ins):
                        done[0] += 1
                        ins.then_inc(spline_chain, 1)
                        pool.wait_ge(spline_chain, done[0])

                    def tt(to, a, b, op):
                        link(nc.gpsimd.tensor_tensor(to, a, b, op))

                    ones = [vg[p][:, :, :, HD:2 * HD] for p in range(2)] + [kb[p][KROWS:KROWS + MROWS] for p in range(2)]
                    for n, rows in enumerate(ones):
                        nc.gpsimd.memset(rows, 1.0).then_inc(ones_ready, 1)
                        pool.wait_ge(ones_ready, n + 1)
                    above, below = (probs[:, n].rearrange("p j s -> p (j s)")[:, 0:B * 2 * E] for n in range(2))
                    raw = gates_raw[:, :, :].rearrange("p b e -> p (b e)")
                    gate = gates[:, :, :, :].rearrange("p b g e -> p (b g e)")
                    pool.wait_ge(vectors_raw, B + 1)
                    link(nc.gpsimd.tensor_scalar(affine[:, 3], affine[:, 3], 1.0, None, ALU.add))
                    link(nc.gpsimd.tensor_scalar(gate, raw, 0.0, None, ALU.is_ge))
                    link(nc.gpsimd.tensor_scalar(above, raw, 0.25, None, ALU.max))
                    tt(above, above, gate, ALU.mult)
                    link(nc.gpsimd.tensor_scalar(gate, gate, -1.0, 1.0, ALU.mult, ALU.add))
                    link(nc.gpsimd.tensor_scalar(below, raw, -0.25, None, ALU.min))
                    tt(below, below, gate, ALU.mult)
                    nc.gpsimd.tensor_tensor(gate, above, below, ALU.add).then_inc(guard_ready, 1)

                    pool.wait_ge(guard_ready, 1)
                    pts, half_pts = windows[:, :, :, :], diff[:, :, :, 0:5]
                    link(nc.gpsimd.tensor_scalar(half_pts, pts, 0.5, None, ALU.mult))
                    d1, d2, d3 = diff[:, :, :, 5:9], diff[:, :, :, 0:3], diff[:, :, :, 3:5]
                    tt(d1, diff[:, :, :, 1:5], diff[:, :, :, 0:4], ALU.subtract)
                    tt(d2, d1[:, :, :, 1:4], d1[:, :, :, 0:3], ALU.subtract)
                    tt(d3, d2[:, :, :, 1:3], d2[:, :, :, 0:2], ALU.subtract)
                    c0 = windows[:, :, :, 1]
                    c1, c2, c3, e2, e3 = (coef[:, n] for n in range(5))
                    tt(c1, d1[:, :, :, 0], d1[:, :, :, 1], ALU.add)
                    tt(c2, d2[:, :, :, 0], d3[:, :, :, 0], ALU.subtract)
                    link(nc.gpsimd.tensor_copy(c3, d3[:, :, :, 0]))
                    tt(e2, d3[:, :, :, 0], d3[:, :, :, 1], ALU.add)
                    tt(e3, d3[:, :, :, 1], d3[:, :, :, 0], ALU.subtract)
                    for q in range(PIECES // 4):
                        m = slice(4 * q, 4 * q + 4)

                        def wide(a):
                            return a.unsqueeze(2).to_broadcast((P, 4, P))

                        tt(z[:, :, :], ramp_sb[:, :].unsqueeze(1).to_broadcast((P, 4, P)), wide(phase_sb[:, m]), ALU.add)
                        link(nc.gpsimd.tensor_scalar(y[:, :, :], z[:, :, :], -1.0, None, ALU.add))
                        link(nc.gpsimd.tensor_scalar(y[:, :, :], y[:, :, :], 0.0, None, ALU.max))
                        for n in range(3):
                            w = spline_w[:, n, m, :]
                            tt(w, z[:, :, :], wide(c3[:, n, m]), ALU.mult)
                            tt(w, w, wide(c2[:, n, m]), ALU.add)
                            tt(w, w, z[:, :, :], ALU.mult)
                            tt(w, w, wide(c1[:, n, m]), ALU.add)
                            tt(w, w, z[:, :, :], ALU.mult)
                            tt(w, w, wide(c0[:, n, m]), ALU.add)
                            tt(bend, y[:, :, :], wide(e3[:, n, m]), ALU.mult)
                            tt(bend, bend, wide(e2[:, n, m]), ALU.subtract)
                            tt(bend, bend, y[:, :, :], ALU.mult)
                            tt(bend, bend, y[:, :, :], ALU.mult)
                            tt(w, w, bend, ALU.add)
                    pool.sem_inc(spline_ready, 1)
                    att_low(0)
                    att_low(1)

        with ExitStack() as mem:
            def sb(name, shape, dt=F32):
                return mem.enter_context(nc.sbuf_tensor(name, shape, dt))

            silu = sb("silu", [P, 2, BLK])
            inter = sb("inter", [P, 2, BLK])
            in_hi = sb("in_hi", [P, IK, BLK], F32R)
            in_lo = sb("in_lo", [P, IK, BLK], F32R)
            ffn = sb("ffn", [P, TPB, E])
            y_sb = sb("y_sb", [P, TPB, E])

            with nc.Block() as block:

                @block.sync
                def _(sp):
                    def store(i):
                        for half in range(2):
                            at = i * BLK + half * 2 * P
                            sp.wait_ge(y_ready, i * 2 + half + 1)
                            sp.dma_start(out[at:at + 2 * P, :].rearrange("(t p) e -> p t e", p=P),
                                         y_sb[:, 2 * half:2 * half + 2, :]).then_inc(y_stored, DMA)

                    sp.wait_ge(heads_ready, GROUPS * HALVES + PV_START)
                    store_heads(GROUPS // 2 - 1, 1)
                    for p in range(2):
                        sp.wait_ge(heads_stored[p], GROUPS // 2 * 2 * GH * DMA + DMA)
                    load_denominators(1)
                    store_inverses(1)
                    for i in range(BLOCKS):
                        if i + 2 < BLOCKS:
                            sp.wait_ge(att_ready, EK * (i + 2))
                            load_att(i + 2, (i + 2) // 2, (i + 2) % 2)
                        store(i)
                    sp.wait_ge(y_stored, 2 * BLOCKS * DMA)

                @block.tensor
                def _(pe):
                    def transpose_block(i):
                        pe.wait_ge(xn_ready, i + 1)
                        for k in range(EK):
                            transpose_tokens(i, k, X_BANK + k)

                    def gate_up(i, chunks):
                        for c in chunks:
                            if c == 0:
                                pe.wait_ge(h_ready, (i + 1) * EK)
                            if c >= 2:
                                pe.wait_ge(inter_ready, i * IK + (c - 1))
                            for g in range(2):
                                for k in range(EK):
                                    for a, (w, x) in enumerate(prod((gu_hi, gu_lo), (h_hi, h_lo))):
                                        last = nc.tensor.matmul(ps[:, G_BANK + 2 * (c % 2) + g, :],
                                                                w[:, g, k, c * P:(c + 1) * P], x[:, k, :],
                                                                start=(k == 0 and a == 0), stop=(k == EK - 1 and a == 2))
                            last.then_inc(gu_made, 1)

                    def down(i, with_next):
                        early, late = range(IK - 2), range(IK - 2, IK)
                        pe.wait_ge(down_read, i * 2 + START)
                        pe.wait_ge(in_ready, i * IK + (IK - 2))
                        for t, chunks in ((0, early), (2, early), (0, late), (1, range(IK)), (2, late), (3, range(IK))):
                            for c in chunks:
                                if t == 0 and c in late:
                                    pe.wait_ge(in_ready, i * IK + (c + 1))
                                for a, (x, w) in enumerate(prod((in_hi, in_lo), (dn_hi, dn_lo))):
                                    last = nc.tensor.matmul(ps[:, D_BANK + t // 2, (t % 2) * E:(t % 2 + 1) * E],
                                                            x[:, c, t * P:(t + 1) * P], w[:, c, :],
                                                            start=(c == 0 and a == 0), stop=(c == IK - 1 and a == 2))
                            if t % 2:
                                last.then_inc(down_made, 1)
                            if with_next and t == 0 and chunks is early:
                                transpose_block(i + 1)

                    with pe.Fori(0, BLOCKS - 1) as i:
                        gate_up(i, range(PROJECT_AT))
                        for t in range(TPB):
                            project_tile(i + 1, t, X_BANK + t // 2)
                        gate_up(i, range(PROJECT_AT, IK))
                        down(i, True)
                    gate_up(BLOCKS - 1, range(IK))
                    down(BLOCKS - 1, False)

                @block.scalar
                def _(act):
                    for i in range(BLOCKS):
                        for c in range(IK):
                            n = i * IK + c
                            act.wait_ge(gu_made, n + 1)
                            if n >= 2:
                                act.wait_ge(inter_ready, n - 1)
                            nc.scalar.activation(silu[:, c % 2], ps[:, G_BANK + 2 * (c % 2), :], ACT.Silu).then_inc(silu_ready, 1)
                            act.wait_ge(inter_ready, n + 1)
                            nc.scalar.copy(in_hi[:, c], inter[:, c % 2]).then_inc(in_hi_ready, 1)
                        if i + 1 < BLOCKS:
                            h_affine(i + 1, (i + 1) // 2)

                @block.gpsimd
                def _(pool):
                    for i in range(BLOCKS):
                        for c in range(IK):
                            n = i * IK + c
                            pool.wait_ge(in_hi_ready, n + 1)
                            nc.gpsimd.tensor_tensor(in_lo[:, c], inter[:, c % 2], in_hi[:, c].bitcast(F32), ALU.subtract)\
                              .then_inc(in_ready, 1)
                        for half in range(2):
                            if i + 2 < BLOCKS:
                                att_low(i + 2, [half])
                            pool.wait_ge(down_read, 2 * i + half + 1 + START)
                            if i and half == 0:
                                pool.wait_ge(y_stored, 2 * i * DMA)
                            nc.gpsimd.tensor_tensor(y_sb[:, 2 * half:2 * half + 2, :], ffn[:, 2 * half:2 * half + 2, :],
                                                    x_sb[:, TPB * i + 2 * half:TPB * i + 2 * half + 2, :], ALU.add)\
                                .then_inc(y_ready, 1)

                @block.vector
                def _(dve):
                    for i in range(BLOCKS):
                        for c in range(IK):
                            n = i * IK + c
                            dve.wait_ge(silu_ready, n + 1)
                            if n >= 2:
                                dve.wait_ge(in_ready, n - 1)
                            nc.vector.tensor_tensor(inter[:, c % 2], silu[:, c % 2], ps[:, G_BANK + 2 * (c % 2) + 1, :],
                                                    ALU.mult).then_inc(inter_ready, 1)
                            if i == 0 and c == IK - 1:
                                invert_denominators(1)
                            if i + 1 < BLOCKS:
                                if c in (PROJECT_AT, PROJECT_AT + 2):
                                    project_gated(i + 1, (i + 1) // 2, (c - PROJECT_AT) // 2)
                                elif c in (PROJECT_AT + 1, PROJECT_AT + 3):
                                    residual(i + 1, (c - PROJECT_AT) // 2)
                                elif c == PROJECT_AT + 4:
                                    inverse_deviation()
                                elif c == PROJECT_AT + 5:
                                    normalise(i + 1)
                        if i + 1 < BLOCKS:
                            h_parts(i + 1)
                        for half in range(2):
                            if i + 2 < BLOCKS:
                                att_high(i + 2, half)
                            dve.wait_ge(down_made, 2 * i + half + 1)
                            if i:
                                dve.wait_ge(y_ready, 2 * (i - 1) + half + 1)
                            nc.vector.tensor_tensor(ffn[:, 2 * half:2 * half + 2, :],
                                                    ps[:, D_BANK + half, :].rearrange("p (t e) -> p t e", t=2),
                                                    gates[:, i // 2, 1, :].unsqueeze(1).to_broadcast((P, 2, E)), ALU.mult)\
                                .then_inc(down_read, 1)


def _spline_grid(np):
    step = (N_CTRL - 1) / (INTER * E - 1)
    column, partition = np.meshgrid(np.arange(PIECES), np.arange(P))
    t = (P * (P * column + partition)) * step
    first = np.floor(t).astype(np.int64)
    assert (first == (P - 1) * column + np.maximum(partition - 1, 0)).all()
    return (t - first).astype(np.float32), (np.arange(P) * step).astype(np.float32)


def kernel(**inputs):
    import numpy as np
    import concourse.bacc as bacc
    from concourse.bass_utils import run_bass_kernel_spmd

    def ends_repeated(cp):
        cp = np.asarray(cp)
        return np.concatenate([cp[:1], cp, cp[-1:], cp[-1:]])

    phase, ramp = _spline_grid(np)
    arrays = {
        "x_in": np.ascontiguousarray(inputs["L0_attn_query"]).reshape(B * S, E),
        "w_qkv": np.ascontiguousarray(inputs["L0_attn_Wqkv"]),
        "b_qkv": np.ascontiguousarray(inputs["L0_attn_bqkv"]),
        "w_proj": np.ascontiguousarray(inputs["L0_attn_Wproj"]),
        "b_proj": np.ascontiguousarray(inputs["L0_attn_bproj"]),
        "gate_cp": ends_repeated(inputs["L0_ffn_gate_cp"]),
        "up_cp": ends_repeated(inputs["L0_ffn_up_cp"]),
        "down_cp": ends_repeated(inputs["L0_ffn_down_cp"]),
        "c_in": np.ascontiguousarray(inputs["L0_c"]),
        "w_mod": np.ascontiguousarray(inputs["L0_wmod"]),
        "phase": phase,
        "ramp": ramp,
    }
    nc = bacc.Bacc("TRN2", target_bir_lowering=False, num_devices=1)
    args = [nc.dram_tensor(name, a.shape, mybir.dt.from_np(a.dtype), kind="ExternalInput").ap()
            for name, a in arrays.items()]
    out = nc.dram_tensor("out", [B * S, E], F32, kind="ExternalOutput").ap()
    adaln_block(nc, *args, out)
    result = run_bass_kernel_spmd(nc, [arrays], core_ids=[0])
    return result.results[0]["out"].reshape(B, S, E)
```
